# Optimizing a Trainium2 kernel written in Bass

```python
import numpy as np
import jax
import jax.numpy as jnp

def _softmax(x, axis=-1):
    return jax.nn.softmax(x, axis=axis)

def _gelu(x):
    return jax.nn.gelu(x, approximate=True)

def _silu(x):
    return jax.nn.silu(x)

def _sigmoid(x):
    return jax.nn.sigmoid(x)

def _layernorm(x, axis=-1, eps=1e-05):
    m = jnp.mean(x, axis=axis, keepdims=True)
    v = jnp.var(x, axis=axis, keepdims=True)
    return (x - m) / jnp.sqrt(v + eps)

def _scatter_add(tgt, idx, src, axis=0):
    return tgt.at[idx].add(src)

def _segment_sum(src, seg, n):
    return jax.ops.segment_sum(src, seg, n)
kernel_name = 'mk_hybrid_d2_jaxref_r8_ecdaae'

def setup_inputs(seed: int=0):
    np.random.seed(seed)
    _w = jnp.asarray

    def _L0_attn_a_setup():
        import jax, jax.numpy as jnp
        import numpy as np
        D_MODEL = 128
        NUM_HEADS = 16
        HEAD_DIM = D_MODEL // NUM_HEADS
        THETA = 10000.0
        B, T = (4, 256)

        def _cos_sin(seq_len, head_dim, theta):
            freqs = 1.0 / theta ** (jnp.arange(0, head_dim, 2, dtype=jnp.float32) / head_dim)
            t = jnp.arange(seq_len, dtype=jnp.float32)
            angles = jnp.outer(t, freqs)
            return jnp.concatenate([jnp.cos(angles), jnp.sin(angles)], axis=-1)

        def _apply_rope(x, cos_sin):
            x1 = x[..., 0::2]
            x2 = x[..., 1::2]
            half = x.shape[-1] // 2
            cos = cos_sin[:, :half]
            sin = cos_sin[:, half:]
            out = jnp.stack([x1 * cos - x2 * sin, x1 * sin + x2 * cos], axis=-1)
            return out.reshape(x.shape)
        key = jax.random.key(seed)
        k1, k2, k3 = jax.random.split(key, 3)
        x = jax.random.normal(k1, (B, T, D_MODEL), dtype=jnp.float32)
        W_qkv = jax.random.normal(k2, (3 * D_MODEL, D_MODEL), dtype=jnp.float32) * D_MODEL ** (-0.5)
        W_out = jax.random.normal(k3, (D_MODEL, D_MODEL), dtype=jnp.float32) * D_MODEL ** (-0.5)
        return {'x': x, 'W_qkv': W_qkv, 'W_out': W_out}
    _L0_attn_a_in = _L0_attn_a_setup()

    def _L0_attn_b_setup():
        import jax, jax.numpy as jnp
        import numpy as np
        NUM_HEAD = 16
        D_Q = 64
        D_KV = 64
        ROPE_BASE = 10000.0

        def _cos_sin(seq_len, dim):
            pos = jnp.arange(seq_len, dtype=jnp.float32)[:, None]
            ids = jnp.arange(dim // 2, dtype=jnp.float32)
            theta = ROPE_BASE ** (-2.0 * ids) / (dim // 2)
            r = pos * theta[None, :]
            return (jnp.cos(r), jnp.sin(r))

        def _rope(x, cos, sin):
            b, s, d = x.shape
            xv = x.reshape(b, s, d // 2, 2)
            x0, x1 = (xv[..., 0], xv[..., 1])
            out = jnp.stack([x0 * cos - x1 * sin, x1 * cos + x0 * sin], axis=-1)
            return out.reshape(b, s, d)
        key = jax.random.key(seed)
        ks = jax.random.split(key, 10)
        d_model, d_q, d_kv = (128, D_Q, D_KV)
        b, s = (2, 256)
        w = lambda k, i, o: jax.random.normal(k, (i, o), dtype=jnp.float32) * 0.02
        return {'x': jax.random.normal(ks[0], (b, s, d_model), dtype=jnp.float32), 'Wd_q_w': w(ks[1], d_model, d_q), 'Wd_q_b': jnp.zeros((d_q,), jnp.float32), 'Wu_q_w': w(ks[2], d_q, d_model), 'Wu_q_b': jnp.zeros((d_model,), jnp.float32), 'Wq_r_w': w(ks[3], d_q, d_model), 'Wq_r_b': jnp.zeros((d_model,), jnp.float32), 'Wk_r_w': w(ks[4], d_model, d_model), 'Wk_r_b': jnp.zeros((d_model,), jnp.float32), 'Wd_kv_w': w(ks[5], d_model, d_kv), 'Wd_kv_b': jnp.zeros((d_kv,), jnp.float32), 'Wu_k_w': w(ks[6], d_kv, d_model), 'Wu_k_b': jnp.zeros((d_model,), jnp.float32), 'Wu_v_w': w(ks[7], d_kv, d_model), 'Wu_v_b': jnp.zeros((d_model,), jnp.float32), 'Wo_w': w(ks[8], d_model, d_model), 'Wo_b': jnp.zeros((d_model,), jnp.float32)}
    _L0_attn_b_in = _L0_attn_b_setup()

    def _L0_ffn_setup():
        import jax, jax.numpy as jnp
        import numpy as np
        DIM = 128
        DEPTH = 6
        HEADS = 16
        DIM_HEAD = 64
        WINDOW = 32
        INNER = HEADS * DIM_HEAD
        DIM_INNER = int(DIM * 4 * 2 / 3)
        QK_SCALE = 8.0

        def shift_tokens(t):
            a, s = jnp.split(t, 2, -1)
            s = jnp.pad(s, ((0, 0), (1, 0), (0, 0)))[:, :-1]
            return jnp.concatenate([a, s], -1)

        def l2norm(t):
            return t / jnp.maximum(jnp.linalg.norm(t, axis=-1, keepdims=True), 1e-12)

        def rotate_half(x):
            x1, x2 = jnp.split(x, 2, -1)
            return jnp.concatenate([-x2, x1], -1)

        def rotary_tables(n):
            half = jnp.arange(0, DIM_HEAD, 2, dtype=jnp.float32)
            inv_freq = 1.0 / 10000.0 ** (half / DIM_HEAD)
            t = jnp.arange(n, dtype=jnp.float32)
            freqs = t[:, None] * inv_freq[None, :]
            freqs = jnp.concatenate([freqs, freqs], -1)
            base_scale = (half + 0.4 * DIM_HEAD) / (1.4 * DIM_HEAD)
            power = (t - n // 2) / (WINDOW // 2)
            scale = base_scale[None, :] ** power[:, None]
            scale = jnp.concatenate([scale, scale], -1)
            return (freqs, scale)

        def local_attention(q, k, v):
            b, h, n, d = q.shape
            w = WINDOW
            nw = n // w
            bq = q.reshape(b, h, nw, w, d)
            bk = k.reshape(b, h, nw, w, d)
            bv = v.reshape(b, h, nw, w, d)

            def look(t):
                p = jnp.pad(t, ((0, 0), (0, 0), (1, 0), (0, 0), (0, 0)))
                return jnp.concatenate([p[:, :, :nw], p[:, :, 1:]], axis=3)
            bk2, bv2 = (look(bk), look(bv))
            seq = jnp.arange(n).reshape(nw, w)
            seq_p = jnp.pad(seq, ((1, 0), (0, 0)), constant_values=-1)
            jt = jnp.concatenate([seq_p[:nw], seq_p[1:]], axis=1)
            it = seq[:, :, None]
            jb = jt[:, None, :]
            mask = (it < jb) | (it > jb + w) | (jb == -1)
            sim = jnp.einsum('bhwie,bhwje->bhwij', bq, bk2) * QK_SCALE
            sim = jnp.where(mask, -jnp.finfo(sim.dtype).max, sim)
            attn = jax.nn.softmax(sim, -1)
            out = jnp.einsum('bhwij,bhwje->bhwie', attn, bv2)
            return out.reshape(b, h, n, d)

        def attn_layer(x, Wqkv, qs, ksc, Wo):
            b, n, _ = x.shape
            qkv = x @ Wqkv
            q, k, v = jnp.split(qkv, 3, -1)
            sh = lambda t: t.reshape(b, n, HEADS, DIM_HEAD).transpose(0, 2, 1, 3)
            q, k, v = (sh(q), sh(k), sh(v))
            q = l2norm(q) * qs
            k = l2norm(k) * ksc
            freqs, scale = rotary_tables(n)
            cos, sin = (jnp.cos(freqs), jnp.sin(freqs))
            q = q * cos * scale + rotate_half(q) * sin * scale
            inv = 1.0 / scale
            k = k * cos * inv + rotate_half(k) * sin * inv
            out = local_attention(q, k, v)
            out = out.transpose(0, 2, 1, 3).reshape(b, n, INNER)
            return out @ Wo

        def ffn_layer(x, g, bln, W1, b1, W2, b2):
            mu = x.mean(-1, keepdims=True)
            var = ((x - mu) ** 2).mean(-1, keepdims=True)
            xn = (x - mu) / jnp.sqrt(var + 1e-05) * g + bln
            hg = xn @ W1 + b1
            a, gate = jnp.split(hg, 2, -1)
            return a * jax.nn.gelu(gate, approximate=False) @ W2 + b2
        key = jax.random.key(seed)
        ks = jax.random.split(key, 8)
        B, N = (2, 256)
        init = lambda k, shape: jax.random.normal(k, shape, jnp.float32) * 0.02
        return {'x': jax.random.normal(ks[0], (B, N, DIM), jnp.float32), 'Wqkv': init(ks[1], (DEPTH, DIM, 3 * INNER)), 'q_scale': jnp.ones((DEPTH, DIM_HEAD), jnp.float32), 'k_scale': jnp.ones((DEPTH, DIM_HEAD), jnp.float32), 'Wo': init(ks[2], (DEPTH, INNER, DIM)), 'ln_g': jnp.ones((DEPTH, DIM), jnp.float32), 'ln_b': jnp.zeros((DEPTH, DIM), jnp.float32), 'W1': init(ks[3], (DEPTH, DIM, 2 * DIM_INNER)), 'b1': jnp.zeros((DEPTH, 2 * DIM_INNER), jnp.float32), 'W2': init(ks[4], (DEPTH, DIM_INNER, DIM)), 'b2': jnp.zeros((DEPTH, DIM), jnp.float32)}
    _L0_ffn_in = _L0_ffn_setup()

    def _L1_attn_a_setup():
        import jax, jax.numpy as jnp
        import numpy as np
        NUM_HEADS = 16
        NEG = -1000000000.0

        def _split_heads(t, h):
            *lead, s, hd = t.shape
            return jnp.swapaxes(t.reshape(*lead, s, h, hd // h), -3, -2)
        key = jax.random.key(seed)
        ks = jax.random.split(key, 5)
        B, S, D = (4, 256, 128)
        scale = 1.0 / np.sqrt(D)
        return {'x': jax.random.normal(ks[0], (B, S, D), dtype=jnp.float32), 'WQ': jax.random.normal(ks[1], (D, D), dtype=jnp.float32) * scale, 'WK': jax.random.normal(ks[2], (D, D), dtype=jnp.float32) * scale, 'WV': jax.random.normal(ks[3], (D, D), dtype=jnp.float32) * scale, 'WO': jax.random.normal(ks[4], (D, D), dtype=jnp.float32) * scale}
    _L1_attn_a_in = _L1_attn_a_setup()

    def _L1_attn_b_setup():
        import jax, jax.numpy as jnp
        import numpy as np
        HEADS = 16
        DIM_HEAD = 64
        SEG = 64
        THETA = 10000.0
        NEG_INF = -1e+30

        def _rotate_half(t):
            t2 = t.reshape(*t.shape[:-1], t.shape[-1] // 2, 2)
            return jnp.stack((-t2[..., 1], t2[..., 0]), axis=-1).reshape(t.shape)
        key = jax.random.key(seed)
        ks = jax.random.split(key, 4)
        b, n, d = (2, 512, 128)
        dim_inner = HEADS * DIM_HEAD
        seq = jax.random.normal(ks[0], (b, n, d), dtype=jnp.float32)
        g_norm = jnp.ones((d,), dtype=jnp.float32)
        W_qkv = jax.random.normal(ks[1], (d, 3 * dim_inner), dtype=jnp.float32) * d ** (-0.5)
        W_out = jax.random.normal(ks[2], (dim_inner, d), dtype=jnp.float32) * dim_inner ** (-0.5)
        pm = jax.random.normal(ks[3], (2, HEADS, 16, DIM_HEAD), dtype=jnp.float32) * 0.02
        return {'seq': seq, 'g_norm': g_norm, 'W_qkv': W_qkv, 'W_out': W_out, 'pm': pm}
    _L1_attn_b_in = _L1_attn_b_setup()

    def _L1_ffn_setup():
        import jax, jax.numpy as jnp
        import numpy as np
        B, S, H, E, K, F = (4, 256, 128, 8, 64, 512)
        key = jax.random.key(seed)
        k0, k1, k2, k3 = jax.random.split(key, 4)
        sc = lambda d: 1.0 / np.sqrt(d).astype(np.float32)
        return {'x': jax.random.normal(k0, (B, S, H), jnp.float32), 'Wg': jax.random.normal(k1, (E, H), jnp.float32) * sc(H), 'W1': jax.random.normal(k2, (E, H, F), jnp.float32) * sc(H), 'b1': jnp.zeros((E, F), jnp.float32), 'W2': jax.random.normal(k3, (E, F, H), jnp.float32) * sc(F), 'b2': jnp.zeros((E, H), jnp.float32)}
    _L1_ffn_in = _L1_ffn_setup()
    _d = {'L0_attn_a_x': _L0_attn_a_in['x'], 'L0_attn_a_W_qkv': _L0_attn_a_in['W_qkv'], 'L0_attn_a_W_out': _L0_attn_a_in['W_out'], 'L0_attn_b_Wd_q_w': _L0_attn_b_in['Wd_q_w'], 'L0_attn_b_Wd_q_b': _L0_attn_b_in['Wd_q_b'], 'L0_attn_b_Wu_q_w': _L0_attn_b_in['Wu_q_w'], 'L0_attn_b_Wu_q_b': _L0_attn_b_in['Wu_q_b'], 'L0_attn_b_Wq_r_w': _L0_attn_b_in['Wq_r_w'], 'L0_attn_b_Wq_r_b': _L0_attn_b_in['Wq_r_b'], 'L0_attn_b_Wk_r_w': _L0_attn_b_in['Wk_r_w'], 'L0_attn_b_Wk_r_b': _L0_attn_b_in['Wk_r_b'], 'L0_attn_b_Wd_kv_w': _L0_attn_b_in['Wd_kv_w'], 'L0_attn_b_Wd_kv_b': _L0_attn_b_in['Wd_kv_b'], 'L0_attn_b_Wu_k_w': _L0_attn_b_in['Wu_k_w'], 'L0_attn_b_Wu_k_b': _L0_attn_b_in['Wu_k_b'], 'L0_attn_b_Wu_v_w': _L0_attn_b_in['Wu_v_w'], 'L0_attn_b_Wu_v_b': _L0_attn_b_in['Wu_v_b'], 'L0_attn_b_Wo_w': _L0_attn_b_in['Wo_w'], 'L0_attn_b_Wo_b': _L0_attn_b_in['Wo_b'], 'L0_ffn_Wqkv': _L0_ffn_in['Wqkv'], 'L0_ffn_q_scale': _L0_ffn_in['q_scale'], 'L0_ffn_k_scale': _L0_ffn_in['k_scale'], 'L0_ffn_Wo': _L0_ffn_in['Wo'], 'L0_ffn_ln_g': _L0_ffn_in['ln_g'], 'L0_ffn_ln_b': _L0_ffn_in['ln_b'], 'L0_ffn_W1': _L0_ffn_in['W1'], 'L0_ffn_b1': _L0_ffn_in['b1'], 'L0_ffn_W2': _L0_ffn_in['W2'], 'L0_ffn_b2': _L0_ffn_in['b2'], 'L1_attn_a_WQ': _L1_attn_a_in['WQ'], 'L1_attn_a_WK': _L1_attn_a_in['WK'], 'L1_attn_a_WV': _L1_attn_a_in['WV'], 'L1_attn_a_WO': _L1_attn_a_in['WO'], 'L1_attn_b_g_norm': _L1_attn_b_in['g_norm'], 'L1_attn_b_W_qkv': _L1_attn_b_in['W_qkv'], 'L1_attn_b_W_out': _L1_attn_b_in['W_out'], 'L1_attn_b_pm': _L1_attn_b_in['pm'], 'L1_ffn_Wg': _L1_ffn_in['Wg'], 'L1_ffn_W1': _L1_ffn_in['W1'], 'L1_ffn_b1': _L1_ffn_in['b1'], 'L1_ffn_W2': _L1_ffn_in['W2'], 'L1_ffn_b2': _L1_ffn_in['b2']}
    _x0 = _d['L0_attn_a_x']
    _d['L0_attn_a_x'] = jax.random.normal(jax.random.fold_in(jax.random.key(seed), 1), (2, 1024, 128), dtype=_x0.dtype)
    del _x0
    return _d

def reference(L0_attn_a_x, L0_attn_a_W_qkv, L0_attn_a_W_out, L0_attn_b_Wd_q_w, L0_attn_b_Wd_q_b, L0_attn_b_Wu_q_w, L0_attn_b_Wu_q_b, L0_attn_b_Wq_r_w, L0_attn_b_Wq_r_b, L0_attn_b_Wk_r_w, L0_attn_b_Wk_r_b, L0_attn_b_Wd_kv_w, L0_attn_b_Wd_kv_b, L0_attn_b_Wu_k_w, L0_attn_b_Wu_k_b, L0_attn_b_Wu_v_w, L0_attn_b_Wu_v_b, L0_attn_b_Wo_w, L0_attn_b_Wo_b, L0_ffn_Wqkv, L0_ffn_q_scale, L0_ffn_k_scale, L0_ffn_Wo, L0_ffn_ln_g, L0_ffn_ln_b, L0_ffn_W1, L0_ffn_b1, L0_ffn_W2, L0_ffn_b2, L1_attn_a_WQ, L1_attn_a_WK, L1_attn_a_WV, L1_attn_a_WO, L1_attn_b_g_norm, L1_attn_b_W_qkv, L1_attn_b_W_out, L1_attn_b_pm, L1_ffn_Wg, L1_ffn_W1, L1_ffn_b1, L1_ffn_W2, L1_ffn_b2):

    def _L0_attn_a_ref(x, W_qkv, W_out):
        import jax, jax.numpy as jnp
        import numpy as np
        D_MODEL = 128
        NUM_HEADS = 16
        HEAD_DIM = D_MODEL // NUM_HEADS
        THETA = 10000.0
        B, T = (4, 256)

        def _cos_sin(seq_len, head_dim, theta):
            freqs = 1.0 / theta ** (jnp.arange(0, head_dim, 2, dtype=jnp.float32) / head_dim)
            t = jnp.arange(seq_len, dtype=jnp.float32)
            angles = jnp.outer(t, freqs)
            return jnp.concatenate([jnp.cos(angles), jnp.sin(angles)], axis=-1)

        def _apply_rope(x, cos_sin):
            x1 = x[..., 0::2]
            x2 = x[..., 1::2]
            half = x.shape[-1] // 2
            cos = cos_sin[:, :half]
            sin = cos_sin[:, half:]
            out = jnp.stack([x1 * cos - x2 * sin, x1 * sin + x2 * cos], axis=-1)
            return out.reshape(x.shape)
        Bsz, Tlen, _ = x.shape
        qkv = jnp.einsum('bti,oi->bto', x, W_qkv)
        qkv = qkv.reshape(Bsz, Tlen, 3 * NUM_HEADS, HEAD_DIM).transpose(0, 2, 1, 3)
        q, k, v = jnp.split(qkv, 3, axis=1)
        cos_sin = _cos_sin(Tlen, HEAD_DIM, THETA)
        q = _apply_rope(q, cos_sin)
        k = _apply_rope(k, cos_sin)
        scores = jnp.einsum('bhqd,bhkd->bhqk', q, k) / np.sqrt(HEAD_DIM).astype(np.float32)
        causal = jnp.tril(jnp.ones((Tlen, Tlen), dtype=bool))
        scores = jnp.where(causal[None, None], scores, -jnp.inf)
        attn = jax.nn.softmax(scores, axis=-1)
        o = jnp.einsum('bhqk,bhkd->bhqd', attn, v)
        o = o.transpose(0, 2, 1, 3).reshape(Bsz, Tlen, D_MODEL)
        return jnp.einsum('bti,oi->bto', o, W_out)

    def _L0_attn_b_ref(x, Wd_q_w, Wd_q_b, Wu_q_w, Wu_q_b, Wq_r_w, Wq_r_b, Wk_r_w, Wk_r_b, Wd_kv_w, Wd_kv_b, Wu_k_w, Wu_k_b, Wu_v_w, Wu_v_b, Wo_w, Wo_b):
        import jax, jax.numpy as jnp
        import numpy as np
        NUM_HEAD = 16
        D_Q = 64
        D_KV = 64
        ROPE_BASE = 10000.0

        def _cos_sin(seq_len, dim):
            pos = jnp.arange(seq_len, dtype=jnp.float32)[:, None]
            ids = jnp.arange(dim // 2, dtype=jnp.float32)
            theta = ROPE_BASE ** (-2.0 * ids) / (dim // 2)
            r = pos * theta[None, :]
            return (jnp.cos(r), jnp.sin(r))

        def _rope(x, cos, sin):
            b, s, d = x.shape
            xv = x.reshape(b, s, d // 2, 2)
            x0, x1 = (xv[..., 0], xv[..., 1])
            out = jnp.stack([x0 * cos - x1 * sin, x1 * cos + x0 * sin], axis=-1)
            return out.reshape(b, s, d)
        b, s, d_model = x.shape
        h = NUM_HEAD
        hd = d_model // h
        scale = jnp.sqrt(jnp.float32(h + D_KV + D_Q))

        def heads(t):
            return t.reshape(b, s, h, hd).transpose(0, 2, 1, 3)
        cos, sin = _cos_sin(s, d_model)
        ct_q = x @ Wd_q_w + Wd_q_b
        qt_c = heads(ct_q @ Wu_q_w + Wu_q_b)
        qt_r = heads(_rope(ct_q @ Wq_r_w + Wq_r_b, cos, sin))
        query = qt_c + qt_r
        ct_kv = x @ Wd_kv_w + Wd_kv_b
        kt_c = heads(ct_kv @ Wu_k_w + Wu_k_b)
        kt_r = heads(_rope(x @ Wk_r_w + Wk_r_b, cos, sin))
        key = kt_c + kt_r
        value = heads(ct_kv @ Wu_v_w + Wu_v_b)
        attn = jnp.einsum('bhqd,bhkd->bhqk', query, key) / scale
        attn = jax.nn.softmax(attn, axis=-1)
        out = jnp.einsum('bhqk,bhkd->bhqd', attn, value)
        out = out.transpose(0, 2, 1, 3).reshape(b, s, d_model)
        return out @ Wo_w + Wo_b

    def _L0_ffn_ref(x, Wqkv, q_scale, k_scale, Wo, ln_g, ln_b, W1, b1, W2, b2):
        import jax, jax.numpy as jnp
        import numpy as np
        DIM = 128
        DEPTH = 6
        HEADS = 16
        DIM_HEAD = 64
        WINDOW = 32
        INNER = HEADS * DIM_HEAD
        DIM_INNER = int(DIM * 4 * 2 / 3)
        QK_SCALE = 8.0

        def shift_tokens(t):
            a, s = jnp.split(t, 2, -1)
            s = jnp.pad(s, ((0, 0), (1, 0), (0, 0)))[:, :-1]
            return jnp.concatenate([a, s], -1)

        def l2norm(t):
            return t / jnp.maximum(jnp.linalg.norm(t, axis=-1, keepdims=True), 1e-12)

        def rotate_half(x):
            x1, x2 = jnp.split(x, 2, -1)
            return jnp.concatenate([-x2, x1], -1)

        def rotary_tables(n):
            half = jnp.arange(0, DIM_HEAD, 2, dtype=jnp.float32)
            inv_freq = 1.0 / 10000.0 ** (half / DIM_HEAD)
            t = jnp.arange(n, dtype=jnp.float32)
            freqs = t[:, None] * inv_freq[None, :]
            freqs = jnp.concatenate([freqs, freqs], -1)
            base_scale = (half + 0.4 * DIM_HEAD) / (1.4 * DIM_HEAD)
            power = (t - n // 2) / (WINDOW // 2)
            scale = base_scale[None, :] ** power[:, None]
            scale = jnp.concatenate([scale, scale], -1)
            return (freqs, scale)

        def local_attention(q, k, v):
            b, h, n, d = q.shape
            w = WINDOW
            nw = n // w
            bq = q.reshape(b, h, nw, w, d)
            bk = k.reshape(b, h, nw, w, d)
            bv = v.reshape(b, h, nw, w, d)

            def look(t):
                p = jnp.pad(t, ((0, 0), (0, 0), (1, 0), (0, 0), (0, 0)))
                return jnp.concatenate([p[:, :, :nw], p[:, :, 1:]], axis=3)
            bk2, bv2 = (look(bk), look(bv))
            seq = jnp.arange(n).reshape(nw, w)
            seq_p = jnp.pad(seq, ((1, 0), (0, 0)), constant_values=-1)
            jt = jnp.concatenate([seq_p[:nw], seq_p[1:]], axis=1)
            it = seq[:, :, None]
            jb = jt[:, None, :]
            mask = (it < jb) | (it > jb + w) | (jb == -1)
            sim = jnp.einsum('bhwie,bhwje->bhwij', bq, bk2) * QK_SCALE
            sim = jnp.where(mask, -jnp.finfo(sim.dtype).max, sim)
            attn = jax.nn.softmax(sim, -1)
            out = jnp.einsum('bhwij,bhwje->bhwie', attn, bv2)
            return out.reshape(b, h, n, d)

        def attn_layer(x, Wqkv, qs, ksc, Wo):
            b, n, _ = x.shape
            qkv = x @ Wqkv
            q, k, v = jnp.split(qkv, 3, -1)
            sh = lambda t: t.reshape(b, n, HEADS, DIM_HEAD).transpose(0, 2, 1, 3)
            q, k, v = (sh(q), sh(k), sh(v))
            q = l2norm(q) * qs
            k = l2norm(k) * ksc
            freqs, scale = rotary_tables(n)
            cos, sin = (jnp.cos(freqs), jnp.sin(freqs))
            q = q * cos * scale + rotate_half(q) * sin * scale
            inv = 1.0 / scale
            k = k * cos * inv + rotate_half(k) * sin * inv
            out = local_attention(q, k, v)
            out = out.transpose(0, 2, 1, 3).reshape(b, n, INNER)
            return out @ Wo

        def ffn_layer(x, g, bln, W1, b1, W2, b2):
            mu = x.mean(-1, keepdims=True)
            var = ((x - mu) ** 2).mean(-1, keepdims=True)
            xn = (x - mu) / jnp.sqrt(var + 1e-05) * g + bln
            hg = xn @ W1 + b1
            a, gate = jnp.split(hg, 2, -1)
            return a * jax.nn.gelu(gate, approximate=False) @ W2 + b2
        for i in range(DEPTH):
            x = attn_layer(shift_tokens(x), Wqkv[i], q_scale[i], k_scale[i], Wo[i]) + x
            x = ffn_layer(shift_tokens(x), ln_g[i], ln_b[i], W1[i], b1[i], W2[i], b2[i]) + x
        return x

    def _L1_attn_a_ref(x, WQ, WK, WV, WO):
        import jax, jax.numpy as jnp
        import numpy as np
        NUM_HEADS = 16
        NEG = -1000000000.0

        def _split_heads(t, h):
            *lead, s, hd = t.shape
            return jnp.swapaxes(t.reshape(*lead, s, h, hd // h), -3, -2)
        h = NUM_HEADS
        S = x.shape[-2]
        Q = _split_heads(x @ WQ.T, h)
        K = _split_heads(x @ WK.T, h)
        V = _split_heads(x @ WV.T, h)
        dk = Q.shape[-1]
        scores = jnp.einsum('bhqd,bhkd->bhqk', Q, K) / jnp.sqrt(jnp.float32(dk))
        causal = jnp.tril(jnp.ones((S, S), dtype=bool))
        scores = jnp.where(causal, scores, NEG)
        m = jnp.max(scores, axis=-1, keepdims=True)
        e = jnp.exp(scores - m)
        attn = e / jnp.sum(e, axis=-1, keepdims=True)
        out = jnp.einsum('bhqk,bhkd->bhqd', attn, V)
        out = jnp.swapaxes(out, -3, -2).reshape(*x.shape[:-1], -1)
        return out @ WO.T

    def _L1_attn_b_ref(seq, g_norm, W_qkv, W_out, pm):
        import jax, jax.numpy as jnp
        import numpy as np
        HEADS = 16
        DIM_HEAD = 64
        SEG = 64
        THETA = 10000.0
        NEG_INF = -1e+30

        def _rotate_half(t):
            t2 = t.reshape(*t.shape[:-1], t.shape[-1] // 2, 2)
            return jnp.stack((-t2[..., 1], t2[..., 0]), axis=-1).reshape(t.shape)
        b, n_tot, dim = seq.shape
        p = pm.shape[2]
        dh = DIM_HEAD
        eps = jnp.asarray(jnp.finfo(seq.dtype).eps, seq.dtype)
        x = seq * jax.lax.rsqrt(jnp.mean(seq * seq, axis=-1, keepdims=True) + eps) * g_norm
        qkv = x @ W_qkv
        q, k, v = jnp.split(qkv, 3, axis=-1)

        def split_heads(t):
            return t.reshape(b, n_tot, HEADS, dh).transpose(0, 2, 1, 3)
        q, k, v = map(split_heads, (q, k, v))
        pos = jnp.arange(n_tot, dtype=seq.dtype)
        inv_freq = 1.0 / THETA ** (jnp.arange(0, dh, 2, dtype=seq.dtype) / dh)
        ang = jnp.repeat(pos[:, None] * inv_freq, 2, axis=-1)
        cos, sin = (jnp.cos(ang), jnp.sin(ang))
        q = q * cos + _rotate_half(q) * sin
        k = k * cos + _rotate_half(k) * sin
        w = n_tot // SEG

        def seg_fold(t):
            return t.reshape(b, HEADS, w, SEG, dh).transpose(0, 2, 1, 3, 4).reshape(b * w, HEADS, SEG, dh)
        q, k, v = map(seg_fold, (q, k, v))
        pmk = jnp.broadcast_to(pm[0], (b * w, HEADS, p, dh))
        pmv = jnp.broadcast_to(pm[1], (b * w, HEADS, p, dh))
        k = jnp.concatenate((pmk, k), axis=-2)
        v = jnp.concatenate((pmv, v), axis=-2)
        scores = jnp.einsum('bhid,bhjd->bhij', q, k) * dh ** (-0.5)
        i = jnp.arange(SEG)[:, None]
        j = jnp.arange(SEG + p)[None, :]
        mask = (j < p) | (j - p <= i)
        scores = jnp.where(mask, scores, NEG_INF)
        attn = jax.nn.softmax(scores, axis=-1)
        out = jnp.einsum('bhij,bhjd->bhid', attn, v)
        out = out.transpose(0, 2, 1, 3).reshape(b * w, SEG, HEADS * dh)
        out = out @ W_out
        return out.reshape(b, n_tot, dim)

    def _L1_ffn_ref(x, Wg, W1, b1, W2, b2):
        import jax, jax.numpy as jnp
        import numpy as np
        B, S, H, E, K, F = (4, 256, 128, 8, 64, 512)
        b, s, h = x.shape
        logits = jnp.einsum('bsh,eh->bse', x, Wg)
        Sm = jnp.swapaxes(jax.nn.softmax(logits, axis=-1), 1, 2)
        G, I = jax.lax.top_k(Sm, K)
        ex = jnp.take_along_axis(x[:, None, :, :], I[..., None], axis=2)
        h1 = jax.nn.gelu(jnp.einsum('bekh,ehf->bekf', ex, W1) + b1[None, :, None, :])
        out = jnp.einsum('bekf,efh->bekh', h1, W2) + b2[None, :, None, :]
        out = G[..., None] * out
        new_x = jnp.zeros_like(x).at[jnp.arange(b)[:, None, None], I].add(out)
        return new_x
    x = L0_attn_a_x
    x = x + _L0_attn_a_ref(_layernorm(x, axis=-1), L0_attn_a_W_qkv, L0_attn_a_W_out)
    x = x + _L0_ffn_ref(_layernorm(x, axis=-1), L0_ffn_Wqkv, L0_ffn_q_scale, L0_ffn_k_scale, L0_ffn_Wo, L0_ffn_ln_g, L0_ffn_ln_b, L0_ffn_W1, L0_ffn_b1, L0_ffn_W2, L0_ffn_b2)
    x = x + _L0_attn_b_ref(_layernorm(x, axis=-1), L0_attn_b_Wd_q_w, L0_attn_b_Wd_q_b, L0_attn_b_Wu_q_w, L0_attn_b_Wu_q_b, L0_attn_b_Wq_r_w, L0_attn_b_Wq_r_b, L0_attn_b_Wk_r_w, L0_attn_b_Wk_r_b, L0_attn_b_Wd_kv_w, L0_attn_b_Wd_kv_b, L0_attn_b_Wu_k_w, L0_attn_b_Wu_k_b, L0_attn_b_Wu_v_w, L0_attn_b_Wu_v_b, L0_attn_b_Wo_w, L0_attn_b_Wo_b)
    x = x + _L0_ffn_ref(_layernorm(x, axis=-1), L0_ffn_Wqkv, L0_ffn_q_scale, L0_ffn_k_scale, L0_ffn_Wo, L0_ffn_ln_g, L0_ffn_ln_b, L0_ffn_W1, L0_ffn_b1, L0_ffn_W2, L0_ffn_b2)
    x = x + _L1_attn_a_ref(_layernorm(x, axis=-1), L1_attn_a_WQ, L1_attn_a_WK, L1_attn_a_WV, L1_attn_a_WO)
    x = x + _L1_ffn_ref(_layernorm(x, axis=-1), L1_ffn_Wg, L1_ffn_W1, L1_ffn_b1, L1_ffn_W2, L1_ffn_b2)
    x = x + _L1_attn_b_ref(_layernorm(x, axis=-1), L1_attn_b_g_norm, L1_attn_b_W_qkv, L1_attn_b_W_out, L1_attn_b_pm)
    x = x + _L1_ffn_ref(_layernorm(x, axis=-1), L1_ffn_Wg, L1_ffn_W1, L1_ffn_b1, L1_ffn_W2, L1_ffn_b2)
    return x

_drawn_inputs = setup_inputs


def setup_inputs(seed=0):
    import zlib

    import numpy as np

    out = dict(_drawn_inputs(seed))
    spreads = {'L0_attn_b_Wd_q_b': (0.0, 0.8),
     'L0_attn_b_Wu_q_b': (0.0, 0.8),
     'L0_attn_b_Wq_r_b': (0.0, 0.8),
     'L0_attn_b_Wk_r_b': (0.0, 2.0),
     'L0_attn_b_Wd_kv_b': (0.0, 0.8),
     'L0_attn_b_Wu_k_b': (0.0, 2.0),
     'L0_attn_b_Wu_v_b': (0.0, 0.604),
     'L0_attn_b_Wo_b': (0.0, 0.1),
     'L0_ffn_q_scale': (1.0, 0.6),
     'L0_ffn_k_scale': (1.0, 0.6),
     'L0_ffn_ln_g': (1.0, 0.6),
     'L0_ffn_ln_b': (0.0, 0.8),
     'L0_ffn_b1': (0.0, 0.42),
     'L0_ffn_b2': (0.0, 0.1),
     'L1_attn_b_g_norm': (1.0, 0.542),
     'L1_ffn_b1': (0.0, 0.532),
     'L1_ffn_b2': (0.0, 0.364)}
    factors = {'L0_attn_b_Wd_q_w': 8.0,
     'L0_attn_b_Wu_q_w': 8.0,
     'L0_attn_b_Wq_r_w': 8.0,
     'L0_attn_b_Wk_r_w': 8.0,
     'L0_attn_b_Wd_kv_w': 8.0,
     'L0_attn_b_Wu_k_w': 8.0,
     'L0_attn_b_Wu_v_w': 8.0,
     'L0_attn_b_Wo_w': 4.495,
     'L1_attn_b_pm': 64.0}
    for name, (base, spread) in spreads.items():
        noise = np.random.default_rng([zlib.crc32(name.encode()), seed]).standard_normal(out[name].shape)
        drawn = base * np.exp(spread * noise) if base else spread * noise
        out[name] = jnp.asarray(drawn.astype(out[name].dtype))
    for name, factor in factors.items():
        out[name] = (out[name] * factor).astype(out[name].dtype)
    return out
```

```python
import concourse.bass as bass
from concourse import mybir
from contextlib import ExitStack
import numpy as np

F32 = mybir.dt.float32
BF16 = mybir.dt.bfloat16
NP_BF16 = mybir.dt.np(BF16)
ACT = mybir.ActivationFunctionType
ALU = mybir.AluOpType
AX = mybir.AxisListType.X

P = 128
DM = 128
BATCH, T = 2, 1024
NT = BATCH * T
CH = 512
NC = NT // CH
LN_EPS = 1e-5
LN_EXP = "natural_log_exp_and_others"


class Signals:

    def __init__(self, nc, names, stage=""):
        self.nc, self.ctx = nc, ExitStack()
        self.sems = {n: self.ctx.enter_context(nc.semaphore(stage + n)) for n in names.split()}

    def __getitem__(self, name):
        return self.sems[name]

    def clear(self):
        for s in self.sems.values():
            self.nc.gpsimd.sem_clear(s)
        self.nc.all_engine_barrier()

    def close(self):
        self.ctx.close()


DEPTH, HEADS, DH = 6, 16, 64
INNER = HEADS * DH
WIN = 32
HP = HEADS // 2
UNITS = 2 * HP
DFF = int(DM * 4 * 2 / 3)
FCH = [(0, 128), (128, 128), (256, DFF - 256)]
QT = 64
NTL = CH // QT
NK = QT + WIN
WA_COLS = UNITS * 256 + INNER
WB_COLS = HP * DM + 2 * DFF + 3 * DM
CC_COLS = 4 + 2 + 6 + 1


def ffn_stack(nc, C, X, wa_d, wb_d, cc_d):
    ctx = ExitStack()
    with ctx:
        def sb(name, shape, dt=F32):
            return ctx.enter_context(nc.sbuf_tensor(C.named(name), shape, dt))

        Z = sb("f_z", [P, NT])
        layernorm(nc, C, X, Z)
        WA = sb("f_wa", [P, WA_COLS])
        WB = sb("f_wb", [P, WB_COLS])
        CC = sb("f_cc", [P, CC_COLS])
        tab = sb("f_tab", [P, 4, T])
        masks = sb("f_masks", [P, 2, 4 * NK], BF16)
        XST = sb("f_xst", [P, 2, WIN + CH])
        Q = sb("f_q", [P, HP, CH])
        K = sb("f_k", [P, HP, WIN + CH])
        V = sb("f_v", [NK, NTL, INNER])
        SQ = sb("f_sq", [P, 2, CH])
        RN = sb("f_rn", [P, 2, CH])
        T1 = sb("f_t1", [P, 2, CH])
        T2 = sb("f_t2", [P, 2, CH])
        T3 = sb("f_t3", [P, 2, CH])
        NM = sb("f_nm", [P, 2, 4])
        RS = sb("f_rs", [P, 2, 4])
        RI = sb("f_ri", [P, 2, 4])
        SB = sb("f_sb", [P, 2, 4, NK])
        PR = sb("f_pr", [P, 2, 4, NK])
        PN = sb("f_pn", [P, 2, 4, NK])
        PT = sb("f_pt", [NK, 2, 4 * P])
        OT = sb("f_ot", [P, 2, HP, QT])
        Y = sb("f_y", [P, 1 + CH])
        YS = sb("f_ys", [P, CH])
        XC = sb("f_xc", [P, CH])
        XN = sb("f_xn", [P, CH])
        SD = sb("f_sd", [P, CH])
        GL = sb("f_gl", [P, 3, CH])
        H = sb("f_h", [P, 3, CH])
        PB = C.banks

        w_qk = WA[:, 0:UNITS * 256].rearrange("p (u r f) -> p u r f", r=2, f=P)
        w_v = WA[:, UNITS * 256:WA_COLS]
        w_o = WB[:, 0:HP * DM].rearrange("p (h f) -> p h f", f=DM)
        w_1 = WB[:, HP * DM:HP * DM + 2 * DFF]
        w_2 = WB[:, HP * DM + 2 * DFF:WB_COLS].rearrange("p (c f) -> p c f", f=DM)

        S = Signals(nc, "w_in tab_in zero_done")
        with nc.Block() as block:
            @block.sync
            def _(sp):
                sp.dma_start(WA[:, :], wa_d[0, :, :]).then_inc(S["w_in"], 16)
                sp.dma_start(WB[:, :], wb_d[0, :, :]).then_inc(S["w_in"], 16)
                sp.dma_start(CC[:, :], cc_d[0, :, :]).then_inc(S["w_in"], 16)
                sp.dma_start(tab[:, :, :], C.f_tab_d).then_inc(S["tab_in"], 16)
                sp.dma_start(masks[:, :, :], C.f_mask_d).then_inc(S["tab_in"], 16)
                sp.wait_ge(S["w_in"], 48)
                sp.wait_ge(S["tab_in"], 32)

            @block.gpsimd
            def _(pool):
                nc.gpsimd.memset(K[:, :, :], 0.0)
        S.clear()
        S.close()

        S = Signals(nc, "xst_done raw_done rot_done nrm_done v_done sq_done ln_done rn_done vev_done "
                        "t1_done t2_done t3_done qk_done kc_done s_done mx_done sub_done exp_done sum_done ri_done "
                        "pn_done pt_done ptev_done pv_done oev_done wo_done yc_done y_done ys_done "
                        "mean_done xc_done sqd_done var_done lnd_done rstd_done xg_done xn_done h1_done gl_done h_done "
                        "z_ps z_done wa_in wb_in xz_done")
        with nc.Fori(0, DEPTH) as layer:
            with nc.Block() as block:

                @block.sync
                def _(sp):
                    sp.wait_ge(S["rot_done"], UNITS * NC)
                    sp.wait_ge(S["v_done"], UNITS * NC)
                    sp.dma_start(WA[:, :], wa_d[bass.ds(layer + 1, 1), :, :].rearrange("a p n -> (a p) n")).then_inc(S["wa_in"], 16)
                    sp.wait_ge(S["z_done"], NC)
                    sp.wait_ge(S["qk_done"], UNITS * NC)
                    sp.dma_start(WB[:, :], wb_d[bass.ds(layer + 1, 1), :, :].rearrange("a p n -> (a p) n")).then_inc(S["wb_in"], 16)
                    sp.dma_start(CC[:, :], cc_d[bass.ds(layer + 1, 1), :, :].rearrange("a p n -> (a p) n")).then_inc(S["wb_in"], 16)
                    sp.wait_ge(S["wa_in"], 16)
                    sp.wait_ge(S["wb_in"], 32)

                @block.tensor
                def _(pe):
                    def norm_sum(s):
                        pe.wait_ge(S["sq_done"], s + 1)
                        if s >= 2:
                            pe.wait_ge(S["ln_done"], s - 1)
                        nc.tensor.matmul(PB[:, 4 + s % 2, :], C.blockones[:, :], SQ[:, s % 2, :],
                                         start=True, stop=True).then_inc(S["nrm_done"], 1)

                    def project(c):
                        for i in range(UNITS):
                            s = UNITS * c + i
                            if i == 0:
                                pe.wait_ge(S["xst_done"], c + 1)
                                if c:
                                    pe.wait_ge(S["z_done"], c)
                            x = XST[:, c % 2, WIN:WIN + CH]
                            if s >= 2:
                                pe.wait_ge(S["t1_done"], s - 1)
                            nc.tensor.matmul(PB[:, s % 2, :], w_qk[:, i, 0, :], x,
                                             start=True, stop=True).then_inc(S["raw_done"], 1)
                            if s >= 2:
                                pe.wait_ge(S["t2_done"], s - 1)
                            nc.tensor.matmul(PB[:, 2 + s % 2, :], w_qk[:, i, 1, :], x,
                                             start=True, stop=True).then_inc(S["rot_done"], 1)
                            t, half = i // 2, i % 2
                            if s >= 2:
                                pe.wait_ge(S["vev_done"], s - 1)
                            nc.tensor.matmul(PB[0:NK, 6 + s % 2, :], XST[:, c % 2, QT * t:QT * t + NK],
                                             w_v[:, half * CH:half * CH + CH],
                                             start=True, stop=True).then_inc(S["v_done"], 1)
                            if i:
                                norm_sum(s - 1)
                        norm_sum(UNITS * c + UNITS - 1)

                    def scores(c, g):
                        n = UNITS * c + g
                        t, half = g // 2, g % 2
                        if g == 0:
                            pe.wait_ge(S["qk_done"], UNITS * (c + 1))
                            if c % 2:
                                pe.wait_ge(S["kc_done"], c // 2 + 1)
                        if n >= 2:
                            pe.wait_ge(S["sub_done"], n - 1)
                        bank = PB[:, n % 2, 0:4 * NK]
                        first = 1 if (c % 2 == 0 and t == 0) else 0
                        nc.tensor.matmul(bank, C.identb[:, :], masks[:, first, :], start=True, stop=False,
                                         skip_group_check=True)
                        for j in range(4):
                            hp = 4 * half + j
                            for a in range(2):
                                last = nc.tensor.matmul(
                                    PB[DH * a:DH * a + DH, n % 2, NK * j:NK * j + NK],
                                    Q[DH * a:DH * a + DH, hp, QT * t:QT * t + QT],
                                    K[DH * a:DH * a + DH, hp, QT * t:QT * t + NK],
                                    start=False, stop=(j == 3), skip_group_check=True)
                        last.then_inc(S["s_done"], 1)

                    def transposes(c, g):
                        n = UNITS * c + g
                        pe.wait_ge(S["pn_done"], n + 1)
                        if n >= 2:
                            pe.wait_ge(S["ptev_done"], n - 1)
                        for j in range(4):
                            last = nc.tensor.transpose(PB[0:NK, 2 + n % 2, P * j:P * j + P], PN[:, n % 2, j, :],
                                                       C.ident[:, :])
                        last.then_inc(S["pt_done"], 1)

                    def values(c, g):
                        n = UNITS * c + g
                        t, half = g // 2, g % 2
                        tile = NTL * c + t
                        pe.wait_ge(S["ptev_done"], n + 1)
                        if g == 0:
                            pe.wait_ge(S["vev_done"], UNITS * (c + 1))
                        if tile >= 2:
                            pe.wait_ge(S["oev_done"], tile - 1)
                        for j in range(4):
                            hp = 4 * half + j
                            for a in range(2):
                                last = nc.tensor.matmul(
                                    PB[DH * a:DH * a + DH, 4 + tile % 2, QT * hp:QT * hp + QT],
                                    V[:, t, P * hp + DH * a:P * hp + DH * a + DH],
                                    PT[:, n % 2, P * j + QT * a:P * j + QT * a + QT],
                                    start=True, stop=True, skip_group_check=True)
                        last.then_inc(S["pv_done"], 1)

                    def out_project(c, t):
                        tile = NTL * c + t
                        pe.wait_ge(S["oev_done"], tile + 1)
                        for hp in range(HP):
                            last = nc.tensor.matmul(PB[:, 6, QT * t:QT * t + QT], w_o[:, hp, :], OT[:, tile % 2, hp, :],
                                                    start=(hp == 0), stop=(hp == HP - 1), skip_group_check=True)
                        last.then_inc(S["wo_done"], 1)

                    def feed_forward(c):
                        pe.wait_ge(S["ys_done"], 2 * (c + 1))
                        nc.tensor.matmul(PB[:, 7, :], C.meanones[:, :], YS[:, :], start=True, stop=True).then_inc(S["mean_done"], 1)
                        pe.wait_ge(S["sqd_done"], c + 1)
                        nc.tensor.matmul(PB[:, 7, :], C.meanones[:, :], SQ[:, 0, :], start=True, stop=True).then_inc(S["var_done"], 1)
                        pe.wait_ge(S["xn_done"], c + 1)
                        for f, (at, n) in enumerate(FCH):
                            nc.tensor.matmul(PB[0:n, 3 + f, :], w_1[:, DFF + at:DFF + at + n], XN[:, :],
                                             start=True, stop=True).then_inc(S["h1_done"], 1)
                            nc.tensor.matmul(PB[0:n, f, :], w_1[:, at:at + n], XN[:, :],
                                             start=True, stop=True).then_inc(S["h1_done"], 1)
                        for f, (at, n) in enumerate(FCH):
                            pe.wait_ge(S["h_done"], 3 * c + f + 1)
                            last = nc.tensor.matmul(PB[:, 6, :], w_2[0:n, f, :], H[0:n, f, :],
                                                    start=(f == 0), stop=(f == 2))
                        last.then_inc(S["z_ps"], 1)

                    for c in range(NC):
                        project(c)
                        for g in range(UNITS + 5):
                            if g < UNITS:
                                scores(c, g)
                            if 2 <= g < UNITS + 2:
                                transposes(c, g - 2)
                            if 3 <= g < UNITS + 3:
                                values(c, g - 3)
                            if g >= 6 and g % 2 == 0:
                                out_project(c, (g - 6) // 2)
                        feed_forward(c)

                @block.scalar
                def _(act):
                    def rsqrt_unit(s):
                        act.wait_ge(S["nrm_done"], s + 1)
                        if s >= 2:
                            act.wait_ge(S["qk_done"], s - 1)
                        nc.scalar.activation(RN[:, s % 2, :], PB[:, 4 + s % 2, :], ACT.Ln, scale=2.0 ** 16,
                                             bias=C.tiny[:, 0:1]).then_inc(S["ln_done"], 1)

                    def rsqrt_end(s):
                        act.wait_ge(S["ln_done"], s + 1)
                        nc.scalar.activation(RN[:, s % 2, :], RN[:, s % 2, :], ACT.Exp, scale=-0.5,
                                             bias=C.ln256[:, 0:1]).then_inc(S["rn_done"], 1)

                    for c in range(NC):
                        nc.scalar.preload_act_table_set(LN_EXP)
                        for i in range(UNITS + 1):
                            s = UNITS * c + i
                            if i < UNITS:
                                act.wait_ge(S["rot_done"], s + 1)
                                if s >= 2:
                                    act.wait_ge(S["nrm_done"], s - 1)
                                nc.scalar.activation(SQ[:, s % 2, :], PB[:, 2 + s % 2, :], ACT.Square).then_inc(S["sq_done"], 1)
                            if i:
                                rsqrt_unit(s - 1)
                            if i < UNITS:
                                act.wait_ge(S["v_done"], s + 1)
                                nc.scalar.copy(V[:, i // 2, (i % 2) * CH:(i % 2) * CH + CH], PB[0:NK, 6 + s % 2, :]).then_inc(S["vev_done"], 1)
                            if i:
                                rsqrt_end(s - 1)
                        for g in range(UNITS + 2):
                            n = UNITS * c + g
                            if g < UNITS:
                                act.wait_ge(S["sub_done"], n + 1)
                                if n >= 2:
                                    act.wait_ge(S["pn_done"], n - 1)
                                nc.scalar.activation(PR[:, n % 2, :, :], SB[:, n % 2, :, :], ACT.Exp).then_inc(S["exp_done"], 1)
                            if g >= 2:
                                m = n - 2
                                act.wait_ge(S["pt_done"], m + 1)
                                if m >= 2:
                                    act.wait_ge(S["pv_done"], m - 1)
                                nc.scalar.copy(PT[:, m % 2, :], PB[0:NK, 2 + m % 2, :]).then_inc(S["ptev_done"], 1)
                        act.wait_ge(S["xc_done"], c + 1)
                        nc.scalar.activation(SQ[:, 0, :], XC[:, :], ACT.Square).then_inc(S["sqd_done"], 1)
                        act.wait_ge(S["var_done"], c + 1)
                        nc.scalar.activation(SD[:, :], PB[:, 7, :], ACT.Ln, bias=C.eps[:, 0:1]).then_inc(S["lnd_done"], 1)
                        act.wait_ge(S["lnd_done"], c + 1)
                        nc.scalar.activation(SD[:, :], SD[:, :], ACT.Exp, scale=-0.5).then_inc(S["rstd_done"], 1)
                        for f, (at, n) in enumerate(FCH):
                            act.wait_ge(S["h1_done"], 6 * c + 2 * f + 1)
                            nc.scalar.activation(GL[0:n, f, :], PB[0:n, 3 + f, :], ACT.Gelu,
                                                 bias=CC[0:n, 9 + f:10 + f]).then_inc(S["gl_done"], 1)

                @block.vector
                def _(dve):
                    def stage_input(c):
                        b = c % 2
                        if c >= 2:
                            dve.wait_ge(S["v_done"], UNITS * (c - 1))
                            dve.wait_ge(S["rot_done"], UNITS * (c - 1))
                        lo, at = (0, CH * c - WIN) if c % 2 else (WIN, CH * c)
                        if c % 2 == 0:
                            nc.vector.memset(XST[0:64, b, 0:WIN], 0.0)
                            nc.vector.memset(XST[64:P, b, 0:WIN + 1], 0.0)
                            nc.vector.tensor_copy(XST[64:P, b, WIN + 1:WIN + CH], Z[64:P, CH * c:CH * c + CH - 1])
                        else:
                            nc.vector.tensor_copy(XST[64:P, b, :], Z[64:P, at - 1:at + WIN + CH - 1])
                        nc.vector.tensor_copy(XST[0:64, b, lo:WIN + CH], Z[0:64, at:at + WIN + CH - lo]).then_inc(S["xst_done"], 1)

                    def finish_unit(c, i):
                        s = UNITS * c + i
                        dve.wait_ge(S["t3_done"], s + 1)
                        dve.wait_ge(S["rn_done"], s + 1)
                        hp = i // 2
                        dst = K[:, hp, WIN:WIN + CH] if i % 2 else Q[:, hp, :]
                        nc.vector.scalar_tensor_tensor(out=dst, in0=RN[:, s % 2, :], scalar=1e12, in1=T3[:, s % 2, :],
                                                       op0=ALU.min, op1=ALU.mult).then_inc(S["qk_done"], 1)

                    stage_input(0)
                    for c in range(NC):
                        for i in range(UNITS + 2):
                            s = UNITS * c + i
                            if i < UNITS:
                                kind, half = i % 2, c % 2
                                if c and i == 0:
                                    dve.wait_ge(S["s_done"], UNITS * c)
                                if c % 2 and i == 0:
                                    dve.wait_ge(S["kc_done"], c // 2 + 1)
                                dve.wait_ge(S["raw_done"], s + 1)
                                if s >= 2:
                                    dve.wait_ge(S["t3_done"], s - 1)
                                nc.vector.scalar_tensor_tensor(
                                    out=T1[:, s % 2, :], in0=PB[:, s % 2, :], scalar=CC[:, 2 * kind:2 * kind + 1],
                                    in1=tab[:, 2 * kind, CH * half:CH * half + CH], op0=ALU.mult, op1=ALU.mult).then_inc(S["t1_done"], 1)
                                dve.wait_ge(S["sq_done"], s + 1)
                                nc.vector.scalar_tensor_tensor(
                                    out=T2[:, s % 2, :], in0=PB[:, 2 + s % 2, :], scalar=CC[:, 2 * kind + 1:2 * kind + 2],
                                    in1=tab[:, 2 * kind + 1, CH * half:CH * half + CH], op0=ALU.mult, op1=ALU.mult).then_inc(S["t2_done"], 1)
                            if i >= 2:
                                finish_unit(c, i - 2)
                        if c + 1 < NC:
                            stage_input(c + 1)
                        for g in range(UNITS + 5):
                            n = UNITS * c + g
                            if g < UNITS:
                                dve.wait_ge(S["s_done"], n + 1)
                                if n >= 2:
                                    dve.wait_ge(S["exp_done"], n - 1)
                                sc = PB[:, n % 2, 0:4 * NK].rearrange("p (j k) -> p j k", k=NK)
                                nc.vector.tensor_reduce(out=NM[:, n % 2, :], in_=sc, axis=AX, op=ALU.max,
                                                        negate=True).then_inc(S["mx_done"], 1)
                            if 1 <= g <= UNITS:
                                m = n - 1
                                dve.wait_ge(S["exp_done"], m + 1)
                                nc.vector.tensor_reduce(out=RS[:, m % 2, :], in_=PR[:, m % 2, :, :], axis=AX,
                                                        op=ALU.add).then_inc(S["sum_done"], 1)
                            if g < UNITS:
                                dve.wait_ge(S["mx_done"], n + 1)
                                nc.vector.tensor_tensor(SB[:, n % 2, :, :], sc,
                                                        NM[:, n % 2, :].rearrange("p (j o) -> p j o", o=1).broadcast_to([P, 4, NK]),
                                                        ALU.add).then_inc(S["sub_done"], 1)
                            if 1 <= g <= UNITS:
                                dve.wait_ge(S["sum_done"], m + 1)
                                if m >= 2:
                                    dve.wait_ge(S["pn_done"], m - 1)
                                nc.vector.reciprocal(RI[:, m % 2, :], RS[:, m % 2, :]).then_inc(S["ri_done"], 1)
                            if g >= 5 and g % 2 == 1:
                                tile = NTL * c + (g - 5) // 2
                                dve.wait_ge(S["pv_done"], 2 * tile + 2)
                                if tile >= 2:
                                    dve.wait_ge(S["wo_done"], tile - 1)
                                nc.vector.tensor_copy(OT[:, tile % 2, :, :], PB[:, 4 + tile % 2, :].rearrange("p (h q) -> p h q", q=QT)).then_inc(S["oev_done"], 1)
                        if c % 2:
                            nc.vector.tensor_copy(Y[:, 0:1], Y[:, CH:CH + 1]).then_inc(S["yc_done"], 1)
                        else:
                            nc.vector.memset(Y[:, 0:1], 0.0).then_inc(S["yc_done"], 1)
                        dve.wait_ge(S["wo_done"], NTL * (c + 1))
                        dve.wait_ge(S["yc_done"], c + 1)
                        nc.vector.tensor_tensor(Y[:, 1:1 + CH], PB[:, 6, :], Z[:, CH * c:CH * c + CH], ALU.add).then_inc(S["y_done"], 1)
                        dve.wait_ge(S["mean_done"], c + 1)
                        nc.vector.tensor_tensor(XC[:, :], YS[:, :], PB[:, 7, :], ALU.subtract).then_inc(S["xc_done"], 1)
                        dve.wait_ge(S["rstd_done"], c + 1)
                        nc.vector.scalar_tensor_tensor(out=XC[:, :], in0=XC[:, :], scalar=CC[:, 4:5], in1=SD[:, :],
                                                       op0=ALU.mult, op1=ALU.mult).then_inc(S["xg_done"], 1)
                        dve.wait_ge(S["xg_done"], c + 1)
                        nc.vector.tensor_scalar(XN[:, :], XC[:, :], CC[:, 5:6], None, ALU.add).then_inc(S["xn_done"], 1)
                        for f, (at, n) in enumerate(FCH):
                            dve.wait_ge(S["gl_done"], 3 * c + f + 1)
                            dve.wait_ge(S["h1_done"], 6 * c + 2 * f + 2)
                            nc.vector.scalar_tensor_tensor(out=H[0:n, f, :], in0=PB[0:n, f, :], scalar=CC[0:n, 6 + f:7 + f],
                                                           in1=GL[0:n, f, :], op0=ALU.add, op1=ALU.mult).then_inc(S["h_done"], 1)
                        dve.wait_ge(S["z_ps"], c + 1)
                        dve.wait_ge(S["y_done"], c + 1)
                        if c + 1 < NC:
                            dve.wait_ge(S["xst_done"], c + 2)
                        nc.vector.scalar_tensor_tensor(out=Z[:, CH * c:CH * c + CH], in0=PB[:, 6, :], scalar=CC[:, 12:13],
                                                       in1=Y[:, 1:1 + CH], op0=ALU.add, op1=ALU.add).then_inc(S["z_done"], 1)

                @block.gpsimd
                def _(pool):
                    for c in range(NC):
                        if c % 2:
                            pool.wait_ge(S["s_done"], UNITS * c)
                            pool.wait_ge(S["ys_done"], 2 * c)
                            nc.gpsimd.tensor_copy(K[:, :, 0:WIN], K[:, :, CH:CH + WIN]).then_inc(S["kc_done"], 1)
                        for i in range(UNITS):
                            s = UNITS * c + i
                            if i == 0 and c:
                                pool.wait_ge(S["ys_done"], 2 * c)
                            pool.wait_ge(S["t1_done"], s + 1)
                            pool.wait_ge(S["t2_done"], s + 1)
                            if s >= 2:
                                pool.wait_ge(S["qk_done"], s - 1)
                            nc.gpsimd.tensor_tensor(T3[:, s % 2, :], T1[:, s % 2, :], T2[:, s % 2, :], ALU.add).then_inc(S["t3_done"], 1)
                        for g in range(UNITS):
                            n = UNITS * c + g
                            pool.wait_ge(S["ri_done"], n + 1)
                            if n >= 2:
                                pool.wait_ge(S["pt_done"], n - 1)
                            nc.gpsimd.tensor_tensor(PN[:, n % 2, :, :], PR[:, n % 2, :, :],
                                                    RI[:, n % 2, :].rearrange("p (j o) -> p j o", o=1).broadcast_to([P, 4, NK]),
                                                    ALU.mult).then_inc(S["pn_done"], 1)
                        pool.wait_ge(S["y_done"], c + 1)
                        if c:
                            pool.wait_ge(S["xc_done"], c)
                        nc.gpsimd.tensor_copy(YS[0:64, :], Y[0:64, 1:1 + CH]).then_inc(S["ys_done"], 1)
                        pool.wait_ge(S["ys_done"], 2 * c + 1)
                        nc.gpsimd.tensor_copy(YS[64:P, :], Y[64:P, 0:CH]).then_inc(S["ys_done"], 1)
            S.clear()
        S.close()

        S = Signals(nc, "sum_done")
        with nc.Block() as block:
            @block.vector
            def _(dve):
                nc.vector.tensor_tensor(X[:, :], X[:, :], Z[:, :], ALU.add)
        S.close()


def layernorm(nc, C, X, out):
    with ExitStack() as ctx:
        XC = ctx.enter_context(nc.sbuf_tensor(C.named("ln_xc"), [P, NC, CH], F32))
        SQ = ctx.enter_context(nc.sbuf_tensor(C.named("ln_sq"), [P, NC, CH], F32))
        SD = ctx.enter_context(nc.sbuf_tensor(C.named("ln_sd"), [P, NC, CH], F32))
        PB = C.banks
        S = Signals(nc, "mean_done xc_done sq_done var_done ln_done rstd_done")
        with nc.Block() as block:
            @block.tensor
            def _(pe):
                for c in range(NC):
                    nc.tensor.matmul(PB[:, c, :], C.meanones[:, :], X[:, CH * c:CH * c + CH],
                                     start=True, stop=True).then_inc(S["mean_done"], 1)
                for c in range(NC):
                    pe.wait_ge(S["sq_done"], c + 1)
                    nc.tensor.matmul(PB[:, 4 + c, :], C.meanones[:, :], SQ[:, c, :],
                                     start=True, stop=True).then_inc(S["var_done"], 1)

            @block.scalar
            def _(act):
                nc.scalar.preload_act_table_set(LN_EXP)
                for c in range(NC):
                    act.wait_ge(S["xc_done"], c + 1)
                    nc.scalar.activation(SQ[:, c, :], XC[:, c, :], ACT.Square).then_inc(S["sq_done"], 1)
                    act.wait_ge(S["var_done"], c + 1)
                    nc.scalar.activation(SD[:, c, :], PB[:, 4 + c, :], ACT.Ln, bias=C.eps[:, 0:1]).then_inc(S["ln_done"], 1)
                    act.wait_ge(S["ln_done"], c + 1)
                    nc.scalar.activation(SD[:, c, :], SD[:, c, :], ACT.Exp, scale=-0.5).then_inc(S["rstd_done"], 1)

            @block.vector
            def _(dve):
                for c in range(NC + 1):
                    if c < NC:
                        dve.wait_ge(S["mean_done"], c + 1)
                        nc.vector.tensor_tensor(XC[:, c, :], X[:, CH * c:CH * c + CH], PB[:, c, :],
                                                ALU.subtract).then_inc(S["xc_done"], 1)
                    if c:
                        d = c - 1
                        dve.wait_ge(S["rstd_done"], d + 1)
                        dve.wait_ge(S["xc_done"], d + 1)
                        nc.vector.tensor_tensor(out[:, CH * d:CH * d + CH], XC[:, d, :], SD[:, d, :], ALU.mult)
        S.clear()
        S.close()


class Consts:
    stage = 0

    def named(self, name):
        return f"{name}_{self.stage}"


def make_consts(nc, ctx, d):
    C = Consts()
    def sb(name, shape, dt=F32):
        return ctx.enter_context(nc.sbuf_tensor(name, shape, dt))
    C.banks = ctx.enter_context(nc.psum_tensor("banks", [P, 8, CH], F32))
    C.ident = sb("c_ident", [P, P])
    C.identb = sb("c_identb", [P, P], BF16)
    C.blockones = sb("c_blockones", [P, P])
    C.meanones = sb("c_meanones", [P, P])
    C.col = sb("c_col", [P, 8])
    C.eps, C.tiny, C.ln256, C.rms_eps = (C.col[:, i:i + 1] for i in range(4))
    S = Signals(nc, "in_done")
    with nc.Block() as block:
        @block.sync
        def _(sp):
            sp.dma_start(C.ident[:, :], d["c_ident"][:, :]).then_inc(S["in_done"], 16)
            sp.dma_start(C.identb[:, :], d["c_identb"][:, :]).then_inc(S["in_done"], 16)
            sp.dma_start(C.blockones[:, :], d["c_blockones"][:, :]).then_inc(S["in_done"], 16)
            sp.wait_ge(S["in_done"], 48)

        @block.vector
        def _(dve):
            nc.vector.memset(C.meanones[:, :], 1.0 / DM)
            for i, v in enumerate((LN_EPS, 2.0 ** -64, float(np.log(256.0)), float(np.finfo(np.float32).eps))):
                nc.vector.memset(C.col[:, i:i + 1], v)
    S.clear()
    S.close()
    return C


def const_arrays():
    bf = NP_BF16
    f = np.float32
    r = {}
    r["c_ident"] = np.eye(P, dtype=f)
    r["c_identb"] = np.eye(P).astype(bf)
    r["c_blockones"] = np.kron(np.eye(2), np.ones((DH, DH))).astype(f)
    half = np.arange(0, DH, 2, dtype=f)
    inv = (f(1.0) / f(10000.0) ** (half / f(DH))).astype(f)
    t = np.arange(T, dtype=f)
    ang = (t[:, None] * inv[None, :]).astype(f).astype(np.float64)
    base = ((half + f(0.4 * DH)) / f(1.4 * DH)).astype(np.float64)
    scale = base[None, :] ** ((t.astype(np.float64) - T // 2) / (WIN // 2))[:, None]
    cos, sin = np.cos(ang), np.sin(ang)
    sgn = np.concatenate([-np.ones(32), np.ones(32)])[:, None]
    two = lambda a: np.concatenate([a, a], 1).T
    rows = [8.0 * two(cos * scale), 8.0 * two(sin * scale) * sgn, two(cos / scale), two(sin / scale) * sgn]
    r["f_tab"] = np.stack([np.concatenate([a, a], 0) for a in rows], 1).astype(f)
    i, j = np.arange(QT)[:, None], np.arange(NK)[None, :]
    ok = (j >= i) & (j <= i + WIN)
    m = np.stack([np.where(ok, 0.0, -1e30), np.where(ok & (j >= WIN), 0.0, -1e30)], 0)
    m = np.tile(m, (1, 2, 4))
    r["f_mask"] = np.ascontiguousarray(m.transpose(1, 0, 2)).astype(bf)
    return r


def ffn_arrays(Wqkv, q_scale, k_scale, Wo, ln_g, ln_b, W1, b1, W2, b2):
    pair = np.concatenate([np.arange(32, 64), np.arange(0, 32)])
    idx = []
    for hp in range(HP):
        for kind in range(2):
            raw = kind * INNER + hp * P + np.arange(P)
            rot = kind * INNER + hp * P + np.concatenate([pair, DH + pair])
            idx += [raw, rot]
    idx = np.concatenate(idx + [2 * INNER + np.arange(INNER)])
    again = lambda a: np.concatenate([a, a[:1]], 0)
    wa = Wqkv[:, :, idx]
    wo = Wo.reshape(DEPTH, HP, P, DM).transpose(0, 2, 1, 3).reshape(DEPTH, P, HP * DM)
    w2 = np.zeros((DEPTH, 3 * P, DM), W2.dtype)
    w2[:, :DFF] = W2
    w2 = w2.reshape(DEPTH, 3, P, DM).transpose(0, 2, 1, 3).reshape(DEPTH, P, 3 * DM)
    wb = np.concatenate([wo, W1, w2], 2)
    cc = np.zeros((DEPTH, P, CC_COLS), W2.dtype)
    twice = lambda a: np.concatenate([a, a], 1)
    cc[:, :, 0], cc[:, :, 1] = twice(q_scale), twice(q_scale[:, pair])
    cc[:, :, 2], cc[:, :, 3] = twice(k_scale), twice(k_scale[:, pair])
    cc[:, :, 4], cc[:, :, 5] = ln_g, ln_b
    for f, (at, n) in enumerate(FCH):
        cc[:, :n, 6 + f] = b1[:, at:at + n]
        cc[:, :n, 9 + f] = b1[:, DFF + at:DFF + at + n]
    cc[:, :, 12] = b2
    return again(wa), again(wb), again(cc)


HD = DM // HEADS
KT = T // P
QCH = T // CH
Q_PARTS, K_PARTS = (0, 0, 1, 0, 2, 1), (0, 1, 0, 2, 0, 1)
ROWS = len(Q_PARTS) * HD
SROWS = ROWS + 3
VW = 32


def small_head_attention(nc, C, X, kind, w_d, tab_d, cols_d, brow_d):
    causal = kind != "latent"
    scale = float(np.float32(1.0) / np.sqrt(np.float32(HEADS + 64 + 64 if kind == "latent" else HD)))
    ctx = ExitStack()
    with ctx:
        def sb(name, shape, dt=F32):
            return ctx.enter_context(nc.sbuf_tensor(C.named(name), shape, dt))

        XN = sb("h_xn", [P, NT])
        layernorm(nc, C, X, XN)
        n_w = w_d.shape[1] // P
        W = sb("h_w", [P, n_w, P])
        COLS = sb("h_cols", [P, 8])
        BROW = sb("h_brow", [1, DM + P])
        tab = sb("h_tab", [P, 2, T])
        selden = sb("h_selden", [P, P])
        maskq = sb("h_maskq", [P, P], BF16)
        maskk = sb("h_maskk", [P, P], BF16)
        XB = sb("h_xb", [P, T])
        CT = sb("h_ct", [P, T])
        T1 = sb("h_t1", [P, 2, CH])
        T2 = sb("h_t2", [P, 2, CH])
        T3 = sb("h_t3", [P, 2, CH])
        QK = sb("h_qk", [P, 2, CH])
        R1 = sb("h_r1", [P, 2, CH])
        PARTS = sb("h_parts", [P, 2, 3, T], BF16)
        QS = sb("h_qs", [P, HP, T], BF16)
        KS = sb("h_ks", [P, HP, T], BF16)
        V = sb("h_v", [P, KT, HEADS, VW])
        NM = sb("h_nm", [P, KT, HEADS])
        NR = sb("h_nr", [P, P])
        NR2 = sb("h_nr2", [P, P])
        NP = sb("h_np", [P, 3, P], BF16)
        E = sb("h_e", [P, 4, 2, CH])
        OS = sb("h_os", [P, 2, CH])
        RD = sb("h_rd", [P, 2, CH])
        ON = sb("h_on", [P, 2, CH])
        PB = C.banks
        parts_s, max_s = C.parts_s, C.max_s

        S = Signals(nc, "in_done")
        with nc.Block() as block:
            @block.sync
            def _(sp):
                sp.dma_start(W[:, :, :], w_d.rearrange("p (n f) -> p n f", f=P)).then_inc(S["in_done"], 16)
                sp.dma_start(COLS[:, :], cols_d[:, :]).then_inc(S["in_done"], 16)
                sp.dma_start(BROW[:, :], brow_d[:, :]).then_inc(S["in_done"], 16)
                sp.dma_start(tab[:, :, :], tab_d[:, :, :]).then_inc(S["in_done"], 16)
                sp.dma_start(selden[:, :], C.d["h_selden"][:, :]).then_inc(S["in_done"], 16)
                sp.dma_start(maskq[:, :], C.d["h_maskq"][:, :]).then_inc(S["in_done"], 16)
                sp.dma_start(maskk[:, :], C.d["h_maskk"][:, :]).then_inc(S["in_done"], 16)
                sp.wait_ge(S["in_done"], 112)

            @block.vector
            def _(dve):
                nc.vector.memset(V[:, :, :, :], 0.0).then_inc(C.v_zero, 1)
                dve.wait_ge(C.v_zero, 1)
                nc.vector.memset(V[:, :, :, HD:HD + 1], 1.0)
                for a in range(2):
                    nc.vector.memset(KS[64 * a + 32:64 * a + 64, :, :], 1.0)
        S.clear()
        nc.gpsimd.sem_clear(C.v_zero)
        nc.all_engine_barrier()
        S.close()

        if kind == "rope":
            w_q, w_qr, w_k, w_kr, w_v = range(5)
            w_out = 5
        elif kind == "plain":
            w_q, w_k, w_v = range(3)
            w_out = 3
        else:
            w_ct, w_qc, w_qr, w_qrr, w_kc, w_kr, w_krr, w_v = range(8)
            w_out = 8

        S1 = Signals(nc, "xb_done ct_ps ct_done a_ps b_ps c_ps t1_done t2_done t3_done qk_done hi_done r1_done mid_done r2_done "
                         "v_ps v_done store_done stack_done", "prep_")
        S2 = Signals(nc, "s_done mx_done nt_done n1_done nr_done n2_done nr2_done n3_done store_done rows_done", "max_")
        S3 = Signals(nc, "st_done exp_done pv_done os_done den_done rd_done on_done y_ps y_done", "soft_")
        with nc.Fori(0, BATCH) as b:
            with nc.Block() as block:
                @block.tensor
                def _(pe):
                    pe.wait_ge(S1["xb_done"], 1)
                    if kind == "latent":
                        for c in range(QCH):
                            nc.tensor.matmul(PB[:, 6 + c, :], W[:, w_ct, :], XB[:, CH * c:CH * c + CH],
                                             start=True, stop=True).then_inc(S1["ct_ps"], 1)
                        pe.wait_ge(S1["ct_done"], QCH)
                    u = 0
                    for which in range(2):
                        for c in range(QCH):
                            at = slice(CH * c, CH * c + CH)
                            if u >= 2:
                                pe.wait_ge(S1["qk_done"], u - 1)
                            if kind == "latent":
                                lo = 64 * which
                                ct = CT[lo:lo + 64, at]
                                nc.tensor.matmul(PB[:, u % 2, :], W[lo:lo + 64, (w_qc, w_kc)[which], :], ct,
                                                 start=True, stop=True).then_inc(S1["c_ps"], 1)
                                if which == 0:
                                    nc.tensor.matmul(PB[:, 2 + u % 2, :], W[0:64, w_qr, :], ct,
                                                     start=True, stop=True).then_inc(S1["a_ps"], 1)
                                    nc.tensor.matmul(PB[:, 4 + u % 2, :], W[0:64, w_qrr, :], ct,
                                                     start=True, stop=True).then_inc(S1["b_ps"], 1)
                                else:
                                    nc.tensor.matmul(PB[:, 2 + u % 2, :], W[:, w_kr, :], XB[:, at],
                                                     start=True, stop=True).then_inc(S1["a_ps"], 1)
                                    nc.tensor.matmul(PB[:, 4 + u % 2, :], W[:, w_krr, :], XB[:, at],
                                                     start=True, stop=True).then_inc(S1["b_ps"], 1)
                            elif kind == "rope":
                                nc.tensor.matmul(PB[:, 2 + u % 2, :], W[:, (w_q, w_k)[which], :], XB[:, at],
                                                 start=True, stop=True).then_inc(S1["a_ps"], 1)
                                nc.tensor.matmul(PB[:, 4 + u % 2, :], W[:, (w_qr, w_kr)[which], :], XB[:, at],
                                                 start=True, stop=True).then_inc(S1["b_ps"], 1)
                            else:
                                nc.tensor.matmul(PB[:, u % 2, :], W[:, (w_q, w_k)[which], :], XB[:, at],
                                                 start=True, stop=True).then_inc(S1["c_ps"], 1)
                            u += 1
                    for t in range(KT):
                        if t >= 2:
                            pe.wait_ge(S1["v_done"], t - 1)
                        bank = PB[:, 6 + t % 2, 0:DM]
                        if kind == "latent":
                            nc.tensor.matmul(bank, CT[64:P, P * t:P * t + P], W[64:P, w_v, :], start=True, stop=False)
                            nc.tensor.matmul(bank, BROW[0:1, DM:DM + P], BROW[0:1, 0:DM], start=False,
                                             stop=True).then_inc(S1["v_ps"], 1)
                        else:
                            nc.tensor.matmul(bank, XB[:, P * t:P * t + P], W[:, w_v, :], start=True,
                                             stop=True).then_inc(S1["v_ps"], 1)

                @block.vector
                def _(dve):
                    nc.vector.tensor_copy(XB[:, :], XN[:, bass.ds(b * T, T)]).then_inc(S1["xb_done"], 1)
                    u = 0
                    for which in range(2):
                        for c in range(QCH):
                            at = slice(CH * c, CH * c + CH)
                            cb = 3 * which
                            if u >= 2:
                                dve.wait_ge(S1["mid_done"], u - 1)
                                dve.wait_ge(S1["r2_done"], u - 1)
                            if kind != "plain":
                                dve.wait_ge(S1["a_ps"], u + 1)
                                nc.vector.scalar_tensor_tensor(out=T1[:, u % 2, :], in0=PB[:, 2 + u % 2, :], scalar=COLS[:, cb:cb + 1],
                                                               in1=tab[:, 0, at], op0=ALU.add, op1=ALU.mult).then_inc(S1["t1_done"], 1)
                                dve.wait_ge(S1["b_ps"], u + 1)
                                nc.vector.scalar_tensor_tensor(out=T2[:, u % 2, :], in0=PB[:, 4 + u % 2, :], scalar=COLS[:, cb + 1:cb + 2],
                                                               in1=tab[:, 1, at], op0=ALU.add, op1=ALU.mult).then_inc(S1["t2_done"], 1)
                                dve.wait_ge(S1["t1_done"], u + 1)
                                dve.wait_ge(S1["t2_done"], u + 1)
                            if kind == "latent":
                                nc.vector.tensor_tensor(T3[:, u % 2, :], T1[:, u % 2, :], T2[:, u % 2, :], ALU.add).then_inc(S1["t3_done"], 1)
                                dve.wait_ge(S1["t3_done"], u + 1)
                                dve.wait_ge(S1["c_ps"], u + 1)
                                nc.vector.scalar_tensor_tensor(out=QK[:, u % 2, :], in0=PB[:, u % 2, :], scalar=COLS[:, cb + 2:cb + 3],
                                                               in1=T3[:, u % 2, :], op0=ALU.add, op1=ALU.add).then_inc(S1["qk_done"], 1)
                            elif kind == "rope":
                                nc.vector.tensor_tensor(QK[:, u % 2, :], T1[:, u % 2, :], T2[:, u % 2, :], ALU.add).then_inc(S1["qk_done"], 1)
                            else:
                                dve.wait_ge(S1["c_ps"], u + 1)
                                nc.vector.tensor_copy(QK[:, u % 2, :], PB[:, u % 2, :]).then_inc(S1["qk_done"], 1)
                            dve.wait_ge(S1["hi_done"], u + 1)
                            nc.vector.tensor_tensor(R1[:, u % 2, :], QK[:, u % 2, :], PARTS[:, which, 0, at], ALU.subtract).then_inc(S1["r1_done"], 1)
                            dve.wait_ge(S1["mid_done"], u + 1)
                            nc.vector.tensor_tensor(PARTS[:, which, 2, at], R1[:, u % 2, :], PARTS[:, which, 1, at], ALU.subtract).then_inc(S1["r2_done"], 1)
                            u += 1

                @block.scalar
                def _(act):
                    if kind == "latent":
                        for c in range(QCH):
                            act.wait_ge(S1["ct_ps"], c + 1)
                            nc.scalar.activation(CT[:, CH * c:CH * c + CH], PB[:, 6 + c, :], ACT.Identity,
                                                 bias=COLS[:, 6:7]).then_inc(S1["ct_done"], 1)
                    u = 0
                    for which in range(2):
                        for c in range(QCH):
                            at = slice(CH * c, CH * c + CH)
                            act.wait_ge(S1["qk_done"], u + 1)
                            nc.scalar.copy(PARTS[:, which, 0, at], QK[:, u % 2, :]).then_inc(S1["hi_done"], 1)
                            act.wait_ge(S1["r1_done"], u + 1)
                            nc.scalar.copy(PARTS[:, which, 1, at], R1[:, u % 2, :]).then_inc(S1["mid_done"], 1)
                            u += 1
                    for t in range(KT):
                        act.wait_ge(S1["v_ps"], t + 1)
                        nc.scalar.copy(V[:, t, :, 0:HD], PB[:, 6 + t % 2, 0:DM].rearrange("p (h d) -> p h d", d=HD)).then_inc(S1["v_done"], 1)

                @block.sync
                def _(sp):
                    for which in range(2):
                        sp.wait_ge(S1["r2_done"], QCH * (which + 1))
                        sp.dma_start(parts_s[which, :, :, :].rearrange("a p t -> p a t"), PARTS[:, which, :, :]).then_inc(S1["store_done"], 16)
                    for which in range(2):
                        sp.wait_ge(S1["store_done"], 32)
                        dst, order = (QS, Q_PARTS) if which == 0 else (KS, K_PARTS)
                        for par in range(2):
                            for slot, part in enumerate(order):
                                row = 64 * par + HD * slot
                                src = parts_s[which, part, :, :].rearrange("(c a d) t -> a d c t", a=2, d=HD)[par]
                                sp.dma_start(dst[row:row + HD, :, :], src).then_inc(S1["stack_done"], 16)
                    sp.wait_ge(S1["stack_done"], 16 * 2 * 2 * len(Q_PARTS))
            S1.clear()

            with nc.Block() as block:
                @block.tensor
                def _(pe):
                    n = 0
                    for qt in range(KT):
                        keys = P * (qt + 1) if causal else T
                        for hp in range(HP):
                            if n >= 2:
                                pe.wait_ge(S2["mx_done"], n - 1)
                            for a in range(2):
                                lo = 64 * a
                                for k0 in range(0, keys, CH):
                                    w = min(CH, keys - k0)
                                    diag = causal and k0 + w == keys
                                    bank = 4 * (n % 2) + 2 * a + k0 // CH
                                    last = nc.tensor.matmul(PB[:, bank, 0:w], QS[lo:lo + ROWS, hp, P * qt:P * qt + P],
                                                            KS[lo:lo + ROWS, hp, k0:k0 + w], start=True, stop=not diag,
                                                            skip_group_check=True)
                                    if diag:
                                        last = nc.tensor.matmul(PB[:, bank, w - P:w], C.identb[:, :], maskq[:, :],
                                                                start=False, stop=True, skip_group_check=True)
                            last.then_inc(S2["s_done"], 1)
                            n += 1
                    pe.wait_ge(S2["mx_done"], n)
                    nc.tensor.transpose(PB[:, 0, 0:P], NM[:, :, :].rearrange("p q h -> p (q h)"), C.ident[:, :]).then_inc(S2["nt_done"], 1)

                @block.vector
                def _(dve):
                    n = 0
                    for qt in range(KT):
                        keys = P * (qt + 1) if causal else T
                        for hp in range(HP):
                            dve.wait_ge(S2["s_done"], n + 1)
                            lo = 4 * (n % 2)
                            sc = PB[:, lo:lo + 4, :].rearrange("p (a c) k -> p a (c k)", a=2)[:, :, 0:keys]
                            nc.vector.tensor_reduce(out=NM[:, qt, 2 * hp:2 * hp + 2], in_=sc, axis=AX, op=ALU.max,
                                                    negate=True).then_inc(S2["mx_done"], 1)
                            n += 1
                    dve.wait_ge(S2["nt_done"], 1)
                    nc.vector.tensor_copy(NR[:, :], PB[:, 0, 0:P]).then_inc(S2["nr_done"], 1)
                    dve.wait_ge(S2["nr_done"], 1)
                    nc.vector.tensor_copy(NP[:, 0, :], NR[:, :]).then_inc(S2["n1_done"], 1)
                    dve.wait_ge(S2["n1_done"], 1)
                    nc.vector.tensor_tensor(NR2[:, :], NR[:, :], NP[:, 0, :], ALU.subtract).then_inc(S2["nr2_done"], 1)
                    dve.wait_ge(S2["nr2_done"], 1)
                    nc.vector.tensor_copy(NP[:, 1, :], NR2[:, :]).then_inc(S2["n2_done"], 1)
                    dve.wait_ge(S2["n2_done"], 1)
                    nc.vector.tensor_tensor(NP[:, 2, :], NR2[:, :], NP[:, 1, :], ALU.subtract).then_inc(S2["n3_done"], 1)

                @block.sync
                def _(sp):
                    sp.wait_ge(S2["n3_done"], 1)
                    sp.dma_start(max_s[:, :, :].rearrange("a r q -> r a q"), NP[:, :, :]).then_inc(S2["store_done"], 16)
                    sp.wait_ge(S2["store_done"], 16)
                    for par in range(2):
                        for part in range(3):
                            row = 64 * par + ROWS + part
                            src = max_s[part, :, :].rearrange("(q c a) n -> a c q n", c=HP, a=2)[par:par + 1]
                            for c in range(HP):
                                sp.dma_start(QS[row:row + 1, c, :].rearrange("o (q n) -> o q n", n=P), src[:, c]).then_inc(S2["rows_done"], 16)
                    sp.wait_ge(S2["rows_done"], 16 * 6 * HP)
            S2.clear()

            quads = [(qc, hg, kt) for qc in range(QCH) for hg in range(4)
                     for kt in range((qc + 1) * CH // P if causal else KT)]
            n_q = len(quads)

            def first_col(qc, kt):
                return max(0, P * kt - CH * qc) if causal else 0

            with nc.Block() as block:
                @block.tensor
                def _(pe):
                    def scores(n):
                        qc, hg, kt = quads[n]
                        c0 = first_col(qc, kt)
                        for a in range(2):
                            m = 2 * n + a
                            hp = 2 * hg + a
                            if m >= 2:
                                pe.wait_ge(S3["exp_done"], m - 1)
                            for h in range(2):
                                lo = 64 * h
                                diag = causal and P * kt >= CH * qc
                                last = nc.tensor.matmul(PB[:, 2 * (m % 2) + h, c0:CH], KS[lo:lo + SROWS, hp, P * kt:P * kt + P],
                                                        QS[lo:lo + SROWS, hp, CH * qc + c0:CH * qc + CH], start=True,
                                                        stop=not diag, skip_group_check=True)
                                if diag:
                                    last = nc.tensor.matmul(PB[:, 2 * (m % 2) + h, c0:c0 + P], C.identb[:, :], maskk[:, :],
                                                            start=False, stop=True, skip_group_check=True)
                            last.then_inc(S3["st_done"], 1)

                    def weigh(n):
                        qc, hg, kt = quads[n]
                        c0 = first_col(qc, kt)
                        grp = 4 * qc + hg
                        pe.wait_ge(S3["exp_done"], 2 * n + 2)
                        if kt == 0 and grp >= 2:
                            pe.wait_ge(S3["os_done"], grp - 1)
                        final = n + 1 == n_q or quads[n + 1][2] == 0
                        for j in range(4):
                            m = 2 * n + j // 2
                            last = nc.tensor.matmul(PB[32 * j:32 * j + 32, 4 + grp % 2, c0:CH], V[:, kt, 4 * hg + j, :],
                                                    E[:, m % 4, j % 2, c0:CH], start=(kt == 0), stop=final,
                                                    skip_group_check=True)
                        last.then_inc(S3["pv_done"], 1)
                        return final

                    def denominators(grp):
                        pe.wait_ge(S3["os_done"], grp + 1)
                        if grp:
                            pe.wait_ge(S3["rd_done"], grp)
                        nc.tensor.matmul(PB[:, 6, :], selden[:, :], OS[:, grp % 2, :], start=True, stop=True).then_inc(S3["den_done"], 1)

                    def project(grp):
                        qc, hg = grp // 4, grp % 4
                        pe.wait_ge(S3["on_done"], grp + 1)
                        if hg == 0 and qc:
                            pe.wait_ge(S3["y_done"], qc)
                        last = nc.tensor.matmul(PB[:, 7, :], W[:, w_out + hg, :], ON[:, grp % 2, :], start=(hg == 0), stop=(hg == 3))
                        last.then_inc(S3["y_ps"], 1)

                    grp = 0
                    todo = []
                    for n in range(n_q + 1):
                        if n < n_q:
                            scores(n)
                        if len(todo) and n >= todo[0][0]:
                            at, what, g = todo.pop(0)
                            what(g)
                        if n and weigh(n - 1):
                            todo += [(n + 2, denominators, grp), (n + 3, project, grp)]
                            grp += 1
                    for at, what, g in todo:
                        what(g)

                @block.scalar
                def _(act):
                    nc.scalar.preload_act_table_set(LN_EXP)
                    for m in range(2 * n_q):
                        qc, hg, kt = quads[m // 2]
                        c0 = first_col(qc, kt)
                        act.wait_ge(S3["st_done"], m + 1)
                        if m >= 4:
                            act.wait_ge(S3["pv_done"], m // 2 - 1)
                        lo = 2 * (m % 2)
                        nc.scalar.activation(E[:, m % 4, :, c0:CH], PB[:, lo:lo + 2, c0:CH], ACT.Exp,
                                             scale=scale).then_inc(S3["exp_done"], 1)

                @block.vector
                def _(dve):
                    done = 0
                    for grp in range(4 * QCH):
                        qc, hg = grp // 4, grp % 4
                        done += (qc + 1) * CH // P if causal else KT
                        dve.wait_ge(S3["pv_done"], done)
                        if grp >= 2:
                            dve.wait_ge(S3["den_done"], grp - 1)
                            dve.wait_ge(S3["on_done"], grp - 1)
                        nc.vector.tensor_copy(OS[:, grp % 2, :], PB[:, 4 + grp % 2, :]).then_inc(S3["os_done"], 1)
                        dve.wait_ge(S3["den_done"], grp + 1)
                        nc.vector.reciprocal(RD[:, grp % 2, :], PB[:, 6, :]).then_inc(S3["rd_done"], 1)
                        dve.wait_ge(S3["rd_done"], grp + 1)
                        if grp >= 2:
                            dve.wait_ge(S3["y_ps"], grp - 1)
                        nc.vector.tensor_tensor(ON[:, grp % 2, :], OS[:, grp % 2, :], RD[:, grp % 2, :], ALU.mult).then_inc(S3["on_done"], 1)
                        if hg == 3:
                            dve.wait_ge(S3["y_ps"], grp + 1)
                            xs = X[:, bass.ds(b * T + CH * qc, CH)]
                            nc.vector.scalar_tensor_tensor(out=xs, in0=PB[:, 7, :], scalar=COLS[:, 7:8], in1=xs,
                                                           op0=ALU.add, op1=ALU.add).then_inc(S3["y_done"], 1)
            S3.clear()
        S1.close()
        S2.close()
        S3.close()


def head_const_arrays():
    bf = NP_BF16
    f = np.float32
    r = {}
    sel = np.zeros((P, P), f)
    for j in range(4):
        sel[32 * j + HD, 32 * j:32 * j + 32] = 1
    r["h_selden"] = sel
    i, j = np.arange(P)[:, None], np.arange(P)[None, :]
    r["h_maskq"] = np.where(j <= i, 0.0, -1e30).astype(bf)
    r["h_maskk"] = np.where(i <= j, 0.0, -1e30).astype(bf)
    sgn = np.tile([-1.0, 1.0], DM // 2)[:, None]
    freqs = (f(1.0) / f(10000.0) ** (np.arange(0, HD, 2, dtype=f) / f(HD))).astype(f)
    ang = np.outer(np.arange(T, dtype=f), freqs).astype(f).astype(np.float64)
    full = lambda a: np.tile(np.repeat(a, 2, 1), (1, HEADS)).T
    r["h_tab0"] = np.stack([full(np.cos(ang)), full(np.sin(ang)) * sgn], 1).astype(f)
    ids = np.arange(DM // 2, dtype=f)
    theta = (f(10000.0) ** (f(-2.0) * ids) / f(DM // 2)).astype(f)
    ang = (np.arange(T, dtype=f)[:, None] * theta[None, :]).astype(f).astype(np.float64)
    full = lambda a: np.repeat(a, 2, 1).T
    r["h_tab1"] = np.stack([full(np.cos(ang)), full(np.sin(ang)) * sgn], 1).astype(f)
    return r


SWAP = np.arange(DM) ^ 1


def out_blocks(Wo):
    blocks = []
    for hg in range(4):
        w = np.zeros((4, 32, DM), Wo.dtype)
        w[:, :HD] = Wo[hg * 32:hg * 32 + 32].reshape(4, HD, DM)
        blocks.append(w.reshape(P, DM))
    return blocks


def rope_arrays(W_qkv, W_out):
    q, k, v = (W_qkv[i * DM:(i + 1) * DM].T for i in range(3))
    w = np.concatenate([q, q[:, SWAP], k, k[:, SWAP], v, *out_blocks(W_out.T)], 1)
    return w, np.zeros((P, 8), w.dtype), np.zeros((1, DM + P), w.dtype)


def plain_arrays(WQ, WK, WV, WO):
    w = np.concatenate([WQ.T, WK.T, WV.T, *out_blocks(WO.T)], 1)
    return w, np.zeros((P, 8), w.dtype), np.zeros((1, DM + P), w.dtype)


def latent_arrays(Wd_q_w, Wd_q_b, Wu_q_w, Wu_q_b, Wq_r_w, Wq_r_b, Wk_r_w, Wk_r_b, Wd_kv_w, Wd_kv_b,
                  Wu_k_w, Wu_k_b, Wu_v_w, Wu_v_b, Wo_w, Wo_b):
    low = lambda a: np.concatenate([a, np.zeros_like(a)], 0)
    high = lambda a: np.concatenate([np.zeros_like(a), a], 0)
    w = np.concatenate([np.concatenate([Wd_q_w, Wd_kv_w], 1), low(Wu_q_w), low(Wq_r_w), low(Wq_r_w[:, SWAP]), high(Wu_k_w),
                        Wk_r_w, Wk_r_w[:, SWAP], high(Wu_v_w), *out_blocks(Wo_w)], 1)
    cols = np.stack([Wq_r_b, Wq_r_b[SWAP], Wu_q_b, Wk_r_b, Wk_r_b[SWAP], Wu_k_b,
                     np.concatenate([Wd_q_b, Wd_kv_b]), Wo_b], 1)
    brow = np.concatenate([Wu_v_b, np.ones(P, Wu_v_b.dtype)])[None, :]
    return w, cols, brow


NE, TOPK, FF = 8, 64, 512
KT = T // P
NP2 = NE // 2
FC = FF // P
BE = BATCH * NE
SLOTS = NE * TOPK


def experts(nc, C, X, wg_d, w1_d, b1_d, w2_d, b2_d):
    ctx = ExitStack()
    with ctx:
        def sb(name, shape, dt=F32):
            return ctx.enter_context(nc.sbuf_tensor(C.named(name), shape, dt))

        XN = sb("m_xn", [P, NT])
        layernorm(nc, C, X, XN)
        WG = sb("m_wg", [P, NE])
        W1 = sb("m_w1", [P, NE, FF])
        W2 = sb("m_w2", [P, NE, FC, DM])
        B1 = sb("m_b1", [P, NE, FC])
        B2 = sb("m_b2", [1, NE * DM])
        ONE = sb("m_one", [BE, TOPK])
        IOTA = sb("m_iota", [P, TOPK])
        KCOL = sb("m_kcol", [P, 1])
        SEL = sb("m_sel", [BE, BATCH, NP2, P], BF16)
        GMASK = sb("m_gmask", [NE, SLOTS])
        XT = sb("m_xt", [P, BATCH, KT, DM])
        L = sb("m_l", [P, KT * BE])
        LM = sb("m_lm", [P, KT * BATCH])
        SM = sb("m_sm", [P, KT, BATCH, NE])
        R = sb("m_r", [BE, 3, T])
        M8 = sb("m_m8", [BE, TOPK])
        ONES = sb("m_ones", [BE, T])
        CMB = sb("m_cmb", [BE, T], BF16)
        CMT = sb("m_cmt", [P, KT, BE])
        OH = sb("m_oh", [P, 4, NE, TOPK])
        EX = sb("m_ex", [P, BATCH, NE, TOPK])
        GM = sb("m_gm", [NE, BATCH, SLOTS])
        GC = sb("m_gc", [P, BATCH * NP2])
        HE = sb("m_he", [P, 2, FC, P])
        OE = sb("m_oe", [P, NP2, BATCH, DM])
        OS = sb("m_os", [P, 4, CH])
        PB = C.banks

        S = Signals(nc, "small_in w1_in w2_in xt_ps xt_done lg_ps l_done lm_done lsub_done lexp_done lsum_done lrec_done sm_done "
                        "r_ps r_done m8_done mr_done pick_done cum_done cm_done ones_done cmt_ps cmt_done oh_done gat_ps ex_done gm_done "
                        "gc_ps gc_done h_ps he_done o_ps oe_done cb_ps os_done sc_ps x_done", "moe_")
        with nc.Block() as block:
            @block.sync
            def _(sp):
                sp.dma_start(WG[:, :], wg_d[:, :]).then_inc(S["small_in"], 16)
                sp.dma_start(B1[:, :, :], b1_d[:, :, :]).then_inc(S["small_in"], 16)
                sp.dma_start(B2[:, :], b2_d[:, :]).then_inc(S["small_in"], 16)
                sp.dma_start(IOTA[:, :], C.d["m_iota"][:, :]).then_inc(S["small_in"], 16)
                sp.dma_start(KCOL[:, :], C.d["m_kcol"][:, :]).then_inc(S["small_in"], 16)
                sp.dma_start(SEL[:, :, :, :], C.d["m_sel"][:, :, :, :]).then_inc(S["small_in"], 16)
                sp.dma_start(GMASK[:, :], C.d["m_gmask"][:, :]).then_inc(S["small_in"], 16)
                sp.dma_start(W1[:, :, :], w1_d.rearrange("e h f -> h e f")).then_inc(S["w1_in"], 16)
                sp.dma_start(W2[:, :, :, :], w2_d.rearrange("e (c p) h -> p e c h", p=P)).then_inc(S["w2_in"], 16)
                sp.wait_ge(S["w1_in"], 16)
                sp.wait_ge(S["w2_in"], 16)

            @block.tensor
            def _(pe):
                pe.wait_ge(S["small_in"], 112)
                for t in range(KT * BATCH):
                    last = nc.tensor.matmul(PB[:, 4, NE * t:NE * t + NE], XN[:, P * t:P * t + P], WG[:, :], start=True, stop=True,
                                            skip_group_check=True)
                last.then_inc(S["lg_ps"], 1)
                for b in range(4):
                    for t in range(4 * b, 4 * b + 4):
                        last = nc.tensor.transpose(PB[:, b, P * (t % 4):P * (t % 4) + P], XN[:, P * t:P * t + P], C.ident[:, :])
                    last.then_inc(S["xt_ps"], 1)
                pe.wait_ge(S["sm_done"], 1)
                for kt in range(KT):
                    last = nc.tensor.transpose(PB[0:BE, 5 + kt // 4, P * (kt % 4):P * (kt % 4) + P],
                                               SM[:, kt, :, :].rearrange("p b e -> p (b e)"), C.ident[:, :])
                last.then_inc(S["r_ps"], 1)
                pe.wait_ge(S["cm_done"], 1)
                pe.wait_ge(S["l_done"], 1)
                for kt in range(KT):
                    last = nc.tensor.matmul(PB[:, 4, BE * kt:BE * kt + BE], CMB[:, P * kt:P * kt + P], C.identb[0:BE, 0:BE],
                                            start=True, stop=True, skip_group_check=True)
                last.then_inc(S["cmt_ps"], 1)
                pe.wait_ge(S["xt_done"], 4)
                pe.wait_ge(S["r_done"], 1)
                for b in range(BATCH):
                    for kt in range(KT):
                        n = KT * b + kt
                        pe.wait_ge(S["oh_done"], n + 1)
                        oh = OH[:, n % 4, :, :].rearrange("p e k -> p (e k)")
                        nc.tensor.matmul(PB[:, b, :], XT[:, b, kt, :], oh, start=(kt == 0), stop=(kt == KT - 1))
                        nc.tensor.matmul(PB[0:NE, 2 + b, :], SM[:, kt, b, :], oh, start=(kt == 0), stop=(kt == KT - 1)).then_inc(S["gat_ps"], 1)
                pe.wait_ge(S["gm_done"], BATCH)
                pe.wait_ge(S["cmt_done"], 1)
                for b in range(BATCH):
                    for e in range(NE):
                        lo, col = 64 * (e % 2), NP2 * b + e // 2
                        last = nc.tensor.matmul(PB[lo:lo + 64, 4, 256 + col:257 + col], GM[:, b, TOPK * e:TOPK * e + TOPK],
                                                ONE[0:NE, 0:1], start=True, stop=True, skip_group_check=True)
                last.then_inc(S["gc_ps"], 1)
                pe.wait_ge(S["ex_done"], BATCH)
                pe.wait_ge(S["w1_in"], 16)
                pe.wait_ge(S["w2_in"], 16)

                def up(e):
                    if e >= 2:
                        pe.wait_ge(S["he_done"], FC * (e - 1))
                    for f in range(FC):
                        last = nc.tensor.matmul(PB[:, 5 + e % 2, P * f:P * f + P], W1[:, e, P * f:P * f + P], EX[:, :, e, :],
                                                start=True, stop=True, skip_group_check=True)
                    last.then_inc(S["h_ps"], 1)

                def down(e):
                    pr, lo = e // 2, 64 * (e % 2)
                    pe.wait_ge(S["he_done"], FC * (e + 1))
                    if pr >= 1 and e % 2 == 0:
                        pe.wait_ge(S["oe_done"], BATCH * pr)
                    for b in range(BATCH):
                        bank = PB[lo:lo + 64, 2 + b, 0:DM]
                        for f in range(FC):
                            nc.tensor.matmul(bank, HE[:, e % 2, f, TOPK * b:TOPK * b + TOPK], W2[:, e, f, :], start=(f == 0),
                                             stop=False, skip_group_check=True)
                        last = nc.tensor.matmul(bank, ONE[0:1, 0:TOPK], B2[0:1, DM * e:DM * e + DM], start=False, stop=True,
                                                skip_group_check=True)
                    last.then_inc(S["o_ps"], 1)

                for e in range(NE + 1):
                    if e < NE:
                        up(e)
                    if e:
                        down(e - 1)
                for b in range(BATCH):
                    for pr in range(NP2 + 1):
                        if pr < NP2:
                            for c in range(2):
                                n = 2 * (NP2 * b + pr) + c
                                if n >= 2:
                                    pe.wait_ge(S["os_done"], n - 1)
                                else:
                                    pe.wait_ge(S["he_done"], FC * NE)
                                nc.tensor.matmul(PB[:, 5 + n % 2, :], SEL[:, b, pr, :], CMB[:, CH * c:CH * c + CH],
                                                 start=True, stop=True).then_inc(S["cb_ps"], 1)
                        if pr:
                            for c in range(2):
                                n = 2 * (NP2 * b + pr - 1) + c
                                pe.wait_ge(S["os_done"], n + 1)
                                pe.wait_ge(S["oe_done"], BATCH * NP2)
                                nc.tensor.matmul(PB[:, 2 * b + c, :], OE[:, pr - 1, b, :], OS[:, n % 4, :], start=(pr == 1),
                                                 stop=(pr == NP2)).then_inc(S["sc_ps"], 1)

            @block.vector
            def _(dve):
                nc.vector.memset(ONES[:, :], 1.0).then_inc(S["ones_done"], 1)
                nc.vector.memset(ONE[:, :], 1.0).then_inc(S["ones_done"], 1)
                dve.wait_ge(S["lg_ps"], 1)
                nc.vector.tensor_copy(L[:, :], PB[:, 4, 0:KT * BE]).then_inc(S["l_done"], 1)
                lg = L[:, :].rearrange("p (t e) -> p t e", e=NE)
                spread = LM[:, :].rearrange("p (t o) -> p t o", o=1).broadcast_to([P, KT * BATCH, NE])
                dve.wait_ge(S["l_done"], 1)
                nc.vector.tensor_reduce(out=LM[:, :], in_=lg, axis=AX, op=ALU.max).then_inc(S["lm_done"], 1)
                dve.wait_ge(S["lm_done"], 1)
                nc.vector.tensor_tensor(lg, lg, spread, ALU.subtract).then_inc(S["lsub_done"], 1)
                dve.wait_ge(S["lexp_done"], 1)
                nc.vector.tensor_reduce(out=LM[:, :], in_=lg, axis=AX, op=ALU.add).then_inc(S["lsum_done"], 1)
                dve.wait_ge(S["lsum_done"], 1)
                nc.vector.reciprocal(LM[:, :], LM[:, :]).then_inc(S["lrec_done"], 1)
                dve.wait_ge(S["lrec_done"], 1)
                nc.vector.tensor_tensor(SM[:, :, :, :].rearrange("p t b e -> p b t e"),
                                        L[:, :].rearrange("p (b t e) -> p b t e", b=BATCH, e=NE),
                                        LM[:, :].rearrange("p (b t o) -> p b t o", b=BATCH, o=1).broadcast_to([P, BATCH, KT, NE]),
                                        ALU.mult).then_inc(S["sm_done"], 1)
                dve.wait_ge(S["r_ps"], 1)
                nc.vector.tensor_copy(R[:, 0, :].rearrange("p (a n) -> p a n", a=2), PB[0:BE, 5:7, :]).then_inc(S["r_done"], 1)
                for r in range(TOPK // 8):
                    dve.wait_ge(S["r_done"], 1)
                    if r:
                        dve.wait_ge(S["mr_done"], r)
                    src = R[:, 0, :] if r == 0 else R[:, 1 + (r - 1) % 2, :]
                    nc.vector.max(M8[:, 8 * r:8 * r + 8], src).then_inc(S["m8_done"], 1)
                    dve.wait_ge(S["m8_done"], r + 1)
                    nc.vector.match_replace(R[:, 1 + r % 2, :], M8[:, 8 * r:8 * r + 8], src, -1.0).then_inc(S["mr_done"], 1)
                dve.wait_ge(S["mr_done"], TOPK // 8)
                end = R[:, 1 + (TOPK // 8 - 1) % 2, :]
                nc.vector.tensor_scalar(R[:, 0, :], end, 0.0, None, ALU.is_lt).then_inc(S["pick_done"], 1)
                dve.wait_ge(S["pick_done"], 1)
                dve.wait_ge(S["ones_done"], 2)
                nc.vector.tensor_tensor_scan(R[:, 1, :], ONES[:, :], R[:, 0, :], 0.0, ALU.mult, ALU.add).then_inc(S["cum_done"], 1)
                dve.wait_ge(S["cum_done"], 1)
                nc.vector.tensor_tensor(CMB[:, :], R[:, 1, :], R[:, 0, :], ALU.mult).then_inc(S["cm_done"], 1)
                dve.wait_ge(S["cmt_ps"], 1)
                nc.vector.tensor_copy(CMT[:, :, :], PB[:, 4, 0:KT * BE].rearrange("p (t r) -> p t r", r=BE)).then_inc(S["cmt_done"], 1)
                dve.wait_ge(S["cmt_done"], 1)
                dve.wait_ge(S["small_in"], 112)
                for b in range(BATCH):
                    for kt in range(KT):
                        n = KT * b + kt
                        if n >= 4:
                            dve.wait_ge(S["gat_ps"], n - 3)
                        nc.vector.tensor_tensor(OH[:, n % 4, :, :],
                                                CMT[:, kt, NE * b:NE * b + NE].rearrange("p (e o) -> p e o", o=1).broadcast_to([P, NE, TOPK]),
                                                IOTA[:, :].rearrange("p (o k) -> p o k", o=1).broadcast_to([P, NE, TOPK]),
                                                ALU.is_equal).then_inc(S["oh_done"], 1)
                for b in range(BATCH):
                    dve.wait_ge(S["gat_ps"], KT * (b + 1))
                    nc.vector.tensor_tensor(GM[:, b, :], PB[0:NE, 2 + b, :], GMASK[:, :], ALU.mult).then_inc(S["gm_done"], 1)
                dve.wait_ge(S["gc_ps"], 1)
                nc.vector.tensor_copy(GC[:, :], PB[:, 4, 256:256 + BATCH * NP2]).then_inc(S["gc_done"], 1)
                dve.wait_ge(S["gc_done"], 1)
                for pr in range(NP2):
                    dve.wait_ge(S["o_ps"], 2 * (pr + 1))
                    for b in range(BATCH):
                        col = NP2 * b + pr
                        nc.vector.tensor_scalar(OE[:, pr, b, :], PB[:, 2 + b, 0:DM], GC[:, col:col + 1], None, ALU.mult).then_inc(S["oe_done"], 1)
                for b in range(BATCH):
                    for pr in range(NP2):
                        for c in range(2):
                            n = 2 * (NP2 * b + pr) + c
                            dve.wait_ge(S["cb_ps"], n + 1)
                            if n >= 4:
                                dve.wait_ge(S["sc_ps"], n - 3)
                            nc.vector.tensor_scalar(OS[:, n % 4, :], PB[:, 5 + n % 2, :], KCOL[:, 0:1], None, ALU.is_equal).then_inc(S["os_done"], 1)
                for b in range(BATCH):
                    for c in range(2):
                        dve.wait_ge(S["sc_ps"], 2 * NP2 * BATCH)
                        at = slice(T * b + CH * c, T * b + CH * c + CH)
                        nc.vector.tensor_tensor(X[:, at], X[:, at], PB[:, 2 * b + c, :], ALU.add).then_inc(S["x_done"], 1)

            @block.scalar
            def _(act):
                act.wait_ge(S["lsub_done"], 1)
                nc.scalar.activation(L[:, :], L[:, :], ACT.Exp).then_inc(S["lexp_done"], 1)
                for b in range(4):
                    act.wait_ge(S["xt_ps"], b + 1)
                    nc.scalar.copy(XT[:, b // 2, 4 * (b % 2):4 * (b % 2) + 4, :], PB[:, b, :].rearrange("p (t f) -> p t f", f=P)).then_inc(S["xt_done"], 1)
                for b in range(BATCH):
                    act.wait_ge(S["gat_ps"], KT * (b + 1))
                    nc.scalar.copy(EX[:, b, :, :], PB[:, b, :].rearrange("p (e k) -> p e k", k=TOPK)).then_inc(S["ex_done"], 1)
                for e in range(NE):
                    act.wait_ge(S["h_ps"], e + 1)
                    if e >= 2:
                        act.wait_ge(S["o_ps"], e - 1)
                    for f in range(FC):
                        nc.scalar.activation(HE[:, e % 2, f, :], PB[:, 5 + e % 2, P * f:P * f + P], ACT.Gelu_apprx_tanh,
                                             bias=B1[:, e, f:f + 1]).then_inc(S["he_done"], 1)
        S.clear()
        S.close()


def expert_const_arrays():
    f = np.float32
    r = {}
    r["m_iota"] = np.tile(np.arange(1, TOPK + 1, dtype=f), (P, 1))
    r["m_kcol"] = np.tile(np.arange(1, TOPK + 1, dtype=f), 2)[:, None]
    sel = np.zeros((BE, BATCH, NP2, 2, TOPK), f)
    for b in range(BATCH):
        for e in range(NE):
            sel[NE * b + e, b, e // 2, e % 2, :] = 1
    r["m_sel"] = sel.reshape(BE, BATCH, NP2, P).astype(NP_BF16)
    r["m_gmask"] = np.kron(np.eye(NE), np.ones((1, TOPK))).astype(f)
    return r


def expert_arrays(Wg, W1, b1, W2, b2):
    return (np.ascontiguousarray(Wg.T), W1, np.ascontiguousarray(b1.reshape(NE, FC, P).transpose(2, 0, 1)), W2, b2.reshape(1, NE * DM))


PM = 16
SK = QT + PM
BCH = T // CH
SEG_W = UNITS * 256 + INNER + HP * DM


def segment_attention(nc, C, X, w_d, g_d, pmk_d, pmv_d):
    ctx = ExitStack()
    with ctx:
        def sb(name, shape, dt=F32):
            return ctx.enter_context(nc.sbuf_tensor(C.named(name), shape, dt))

        XN = sb("s_xn", [P, NT])
        layernorm(nc, C, X, XN)
        G = sb("s_g", [P, 1])
        W = sb("s_w", [P, SEG_W])
        tab = sb("s_tab", [P, 4, T])
        mask = sb("s_mask", [P, 4 * SK], BF16)
        PMK = sb("s_pmk", [P, HP, PM])
        XB = sb("s_xb", [P, T])
        Q = sb("s_q", [P, HP, CH])
        K = sb("s_k", [P, HP, CH])
        V = sb("s_v", [SK, NTL, INNER])
        T1 = sb("s_t1", [P, 2, CH])
        T2 = sb("s_t2", [P, 2, CH])
        NM = sb("s_nm", [P, 2, 4])
        RS = sb("s_rs", [P, 2, 4])
        RI = sb("s_ri", [P, 2, 4])
        SB = sb("s_sb", [P, 2, 4, SK])
        PR = sb("s_pr", [P, 2, 4, SK])
        PN = sb("s_pn", [P, 2, 4, SK])
        PT = sb("s_pt", [SK, 2, 4 * P])
        OT = sb("s_ot", [P, 2, HP, QT])
        PB = C.banks
        w_qk = W[:, 0:UNITS * 256].rearrange("p (u r f) -> p u r f", r=2, f=P)
        w_v = W[:, UNITS * 256:UNITS * 256 + INNER]
        w_o = W[:, UNITS * 256 + INNER:SEG_W].rearrange("p (h f) -> p h f", f=DM)

        S = Signals(nc, "in_done sq_done ms_done ln_done rs_done", "seg_in_")
        with nc.Block() as block:
            @block.sync
            def _(sp):
                sp.dma_start(G[:, :], g_d[:, :]).then_inc(S["in_done"], 16)
                sp.dma_start(W[:, :], w_d[:, :]).then_inc(S["in_done"], 16)
                sp.dma_start(tab[:, :, :], C.d["s_tab"][:, :, :]).then_inc(S["in_done"], 16)
                sp.dma_start(mask[:, :], C.d["s_mask"][:, :]).then_inc(S["in_done"], 16)
                sp.dma_start(PMK[:, :, :], pmk_d[:, :, :]).then_inc(S["in_done"], 16)
                for t in range(NTL):
                    sp.dma_start(V[QT:SK, t, :], pmv_d[:, :]).then_inc(S["in_done"], 16)
                sp.wait_ge(S["in_done"], 16 * (5 + NTL))

            @block.tensor
            def _(pe):
                for c in range(NC):
                    pe.wait_ge(S["sq_done"], c + 1)
                    if c >= 2:
                        pe.wait_ge(S["ln_done"], c - 1)
                    nc.tensor.matmul(PB[:, c % 2, :], C.meanones[:, :], spare(Q, c), start=True, stop=True).then_inc(S["ms_done"], 1)

            @block.scalar
            def _(act):
                nc.scalar.preload_act_table_set(LN_EXP)
                for c in range(NC):
                    nc.scalar.activation(spare(Q, c), XN[:, CH * c:CH * c + CH], ACT.Square).then_inc(S["sq_done"], 1)
                for c in range(NC):
                    act.wait_ge(S["ms_done"], c + 1)
                    nc.scalar.activation(spare(K, c), PB[:, c % 2, :], ACT.Ln, bias=C.rms_eps[:, 0:1]).then_inc(S["ln_done"], 1)
                    act.wait_ge(S["ln_done"], c + 1)
                    nc.scalar.activation(spare(K, c), spare(K, c), ACT.Exp, scale=-0.5).then_inc(S["rs_done"], 1)

            @block.vector
            def _(dve):
                dve.wait_ge(S["in_done"], 16 * (5 + NTL))
                for c in range(NC):
                    dve.wait_ge(S["rs_done"], c + 1)
                    at = slice(CH * c, CH * c + CH)
                    nc.vector.scalar_tensor_tensor(out=XN[:, at], in0=XN[:, at], scalar=G[:, 0:1], in1=spare(K, c),
                                                   op0=ALU.mult, op1=ALU.mult)
        S.clear()
        S.close()

        S = Signals(nc, "xb_done raw_done rot_done v_done vev_done t1_done t2_done qk_done s_done mx_done sub_done exp_done sum_done "
                        "ri_done pn_done pt_done ptev_done pv_done oev_done wo_done y_done", "seg_")
        with nc.Fori(0, BATCH) as b:
            with nc.Block() as block:
                @block.tensor
                def _(pe):
                    def project(c):
                        for i in range(UNITS):
                            s = UNITS * c + i
                            x = XB[:, CH * c:CH * c + CH]
                            if i == 0:
                                pe.wait_ge(S["xb_done"], 1)
                                if c:
                                    pe.wait_ge(S["y_done"], c)
                            if s >= 2:
                                pe.wait_ge(S["t1_done"], s - 1)
                            nc.tensor.matmul(PB[:, s % 2, :], w_qk[:, i, 0, :], x, start=True, stop=True).then_inc(S["raw_done"], 1)
                            if s >= 2:
                                pe.wait_ge(S["t2_done"], s - 1)
                            nc.tensor.matmul(PB[:, 2 + s % 2, :], w_qk[:, i, 1, :], x, start=True, stop=True).then_inc(S["rot_done"], 1)
                            t, half = i // 2, i % 2
                            if s >= 2:
                                pe.wait_ge(S["vev_done"], s - 1)
                            at = CH * c + QT * t
                            nc.tensor.matmul(PB[0:QT, 6 + s % 2, :], XB[:, at:at + QT], w_v[:, half * CH:half * CH + CH],
                                             start=True, stop=True).then_inc(S["v_done"], 1)

                    def scores(c, g):
                        n = UNITS * c + g
                        t, half = g // 2, g % 2
                        if g == 0:
                            pe.wait_ge(S["qk_done"], UNITS * (c + 1))
                        if n >= 2:
                            pe.wait_ge(S["sub_done"], n - 1)
                        nc.tensor.matmul(PB[:, n % 2, 0:4 * SK], C.identb[:, :], mask[:, :], start=True, stop=False,
                                         skip_group_check=True)
                        for j in range(4):
                            hp = 4 * half + j
                            for a in range(2):
                                lo = DH * a
                                nc.tensor.matmul(PB[lo:lo + DH, n % 2, SK * j:SK * j + QT],
                                                 Q[lo:lo + DH, hp, QT * t:QT * t + QT], K[lo:lo + DH, hp, QT * t:QT * t + QT],
                                                 start=False, stop=False, skip_group_check=True)
                            for a in range(2):
                                lo = DH * a
                                last = nc.tensor.matmul(PB[lo:lo + DH, n % 2, SK * j + QT:SK * j + SK],
                                                        Q[lo:lo + DH, hp, QT * t:QT * t + QT], PMK[lo:lo + DH, hp, :],
                                                        start=False, stop=(j == 3), skip_group_check=True)
                        last.then_inc(S["s_done"], 1)

                    def transposes(c, g):
                        n = UNITS * c + g
                        pe.wait_ge(S["pn_done"], n + 1)
                        if n >= 2:
                            pe.wait_ge(S["ptev_done"], n - 1)
                        for j in range(4):
                            last = nc.tensor.transpose(PB[0:SK, 2 + n % 2, P * j:P * j + P], PN[:, n % 2, j, :], C.ident[:, :])
                        last.then_inc(S["pt_done"], 1)

                    def values(c, g):
                        n = UNITS * c + g
                        t, half = g // 2, g % 2
                        tile = NTL * c + t
                        pe.wait_ge(S["ptev_done"], n + 1)
                        if g == 0:
                            pe.wait_ge(S["vev_done"], UNITS * (c + 1))
                        if tile >= 2:
                            pe.wait_ge(S["oev_done"], tile - 1)
                        for j in range(4):
                            hp = 4 * half + j
                            for a in range(2):
                                last = nc.tensor.matmul(
                                    PB[DH * a:DH * a + DH, 4 + tile % 2, QT * hp:QT * hp + QT],
                                    V[:, t, P * hp + DH * a:P * hp + DH * a + DH],
                                    PT[:, n % 2, P * j + QT * a:P * j + QT * a + QT], start=True, stop=True, skip_group_check=True)
                        last.then_inc(S["pv_done"], 1)

                    def out_project(c, t):
                        tile = NTL * c + t
                        pe.wait_ge(S["oev_done"], tile + 1)
                        if t == 0:
                            pe.wait_ge(S["vev_done"], UNITS * (c + 1))
                        for hp in range(HP):
                            last = nc.tensor.matmul(PB[:, 6, QT * t:QT * t + QT], w_o[:, hp, :], OT[:, tile % 2, hp, :],
                                                    start=(hp == 0), stop=(hp == HP - 1), skip_group_check=True)
                        last.then_inc(S["wo_done"], 1)

                    for c in range(BCH):
                        project(c)
                        for g in range(UNITS + 5):
                            if g < UNITS:
                                scores(c, g)
                            if 2 <= g < UNITS + 2:
                                transposes(c, g - 2)
                            if 3 <= g < UNITS + 3:
                                values(c, g - 3)
                            if g >= 6 and g % 2 == 0:
                                out_project(c, (g - 6) // 2)

                @block.scalar
                def _(act):
                    nc.scalar.preload_act_table_set(LN_EXP)
                    for c in range(BCH):
                        for i in range(UNITS):
                            s = UNITS * c + i
                            act.wait_ge(S["v_done"], s + 1)
                            if c and i == 0:
                                act.wait_ge(S["pv_done"], UNITS * c)
                            nc.scalar.copy(V[0:QT, i // 2, (i % 2) * CH:(i % 2) * CH + CH], PB[0:QT, 6 + s % 2, :]).then_inc(S["vev_done"], 1)
                        for g in range(UNITS + 2):
                            n = UNITS * c + g
                            if g < UNITS:
                                act.wait_ge(S["sub_done"], n + 1)
                                if n >= 2:
                                    act.wait_ge(S["pn_done"], n - 1)
                                nc.scalar.activation(PR[:, n % 2, :, :], SB[:, n % 2, :, :], ACT.Exp).then_inc(S["exp_done"], 1)
                            if g >= 2:
                                m = n - 2
                                act.wait_ge(S["pt_done"], m + 1)
                                if m >= 2:
                                    act.wait_ge(S["pv_done"], m - 1)
                                nc.scalar.copy(PT[:, m % 2, :], PB[0:SK, 2 + m % 2, :]).then_inc(S["ptev_done"], 1)

                @block.vector
                def _(dve):
                    nc.vector.tensor_copy(XB[:, :], XN[:, bass.ds(b * T, T)]).then_inc(S["xb_done"], 1)
                    for c in range(BCH):
                        for i in range(UNITS):
                            s = UNITS * c + i
                            kind = i % 2
                            if c and i == 0:
                                dve.wait_ge(S["s_done"], UNITS * c)
                            dve.wait_ge(S["raw_done"], s + 1)
                            if s >= 2:
                                dve.wait_ge(S["qk_done"], s - 1)
                            at = slice(CH * c, CH * c + CH)
                            nc.vector.tensor_tensor(T1[:, s % 2, :], PB[:, s % 2, :], tab[:, 2 * kind, at], ALU.mult).then_inc(S["t1_done"], 1)
                            dve.wait_ge(S["rot_done"], s + 1)
                            nc.vector.tensor_tensor(T2[:, s % 2, :], PB[:, 2 + s % 2, :], tab[:, 2 * kind + 1, at], ALU.mult).then_inc(S["t2_done"], 1)
                        for g in range(UNITS + 5):
                            n = UNITS * c + g
                            if g < UNITS:
                                dve.wait_ge(S["s_done"], n + 1)
                                if n >= 2:
                                    dve.wait_ge(S["exp_done"], n - 1)
                                sc = PB[:, n % 2, 0:4 * SK].rearrange("p (j k) -> p j k", k=SK)
                                nc.vector.tensor_reduce(out=NM[:, n % 2, :], in_=sc, axis=AX, op=ALU.max,
                                                        negate=True).then_inc(S["mx_done"], 1)
                            if 1 <= g <= UNITS:
                                m = n - 1
                                dve.wait_ge(S["exp_done"], m + 1)
                                nc.vector.tensor_reduce(out=RS[:, m % 2, :], in_=PR[:, m % 2, :, :], axis=AX,
                                                        op=ALU.add).then_inc(S["sum_done"], 1)
                            if g < UNITS:
                                dve.wait_ge(S["mx_done"], n + 1)
                                nc.vector.tensor_tensor(SB[:, n % 2, :, :], sc,
                                                        NM[:, n % 2, :].rearrange("p (j o) -> p j o", o=1).broadcast_to([P, 4, SK]),
                                                        ALU.add).then_inc(S["sub_done"], 1)
                            if 1 <= g <= UNITS:
                                dve.wait_ge(S["sum_done"], m + 1)
                                if m >= 2:
                                    dve.wait_ge(S["pn_done"], m - 1)
                                nc.vector.reciprocal(RI[:, m % 2, :], RS[:, m % 2, :]).then_inc(S["ri_done"], 1)
                            if g >= 5 and g % 2 == 1:
                                tile = NTL * c + (g - 5) // 2
                                dve.wait_ge(S["pv_done"], 2 * tile + 2)
                                if tile >= 2:
                                    dve.wait_ge(S["wo_done"], tile - 1)
                                nc.vector.tensor_copy(OT[:, tile % 2, :, :], PB[:, 4 + tile % 2, :].rearrange("p (h q) -> p h q", q=QT)).then_inc(S["oev_done"], 1)
                        dve.wait_ge(S["wo_done"], NTL * (c + 1))
                        xs = X[:, bass.ds(b * T + CH * c, CH)]
                        nc.vector.tensor_tensor(xs, PB[:, 6, :], xs, ALU.add).then_inc(S["y_done"], 1)

                @block.gpsimd
                def _(pool):
                    for c in range(BCH):
                        for i in range(UNITS):
                            s = UNITS * c + i
                            pool.wait_ge(S["t1_done"], s + 1)
                            pool.wait_ge(S["t2_done"], s + 1)
                            dst = (K if i % 2 else Q)[:, i // 2, :]
                            nc.gpsimd.tensor_tensor(dst, T1[:, s % 2, :], T2[:, s % 2, :], ALU.add).then_inc(S["qk_done"], 1)
                        for g in range(UNITS):
                            n = UNITS * c + g
                            pool.wait_ge(S["ri_done"], n + 1)
                            if n >= 2:
                                pool.wait_ge(S["pt_done"], n - 1)
                            nc.gpsimd.tensor_tensor(PN[:, n % 2, :, :], PR[:, n % 2, :, :],
                                                    RI[:, n % 2, :].rearrange("p (j o) -> p j o", o=1).broadcast_to([P, 4, SK]),
                                                    ALU.mult).then_inc(S["pn_done"], 1)
            S.clear()
        S.close()


def spare(tile, c):
    return tile[:, c, :]


def segment_const_arrays():
    f = np.float32
    r = {}
    inv = (f(1.0) / f(10000.0) ** (np.arange(0, DH, 2, dtype=f) / f(DH))).astype(f)
    ang = (np.arange(T, dtype=f)[:, None] * inv).astype(f).astype(np.float64)
    sgn = np.tile([-1.0, 1.0], DM // 2)[:, None]
    full = lambda a: np.tile(np.repeat(a, 2, 1), (1, 2)).T
    c, s = full(np.cos(ang)), full(np.sin(ang)) * sgn
    r["s_tab"] = np.stack([c / 8.0, s / 8.0, c, s], 1).astype(f)
    i, j = np.arange(QT)[:, None], np.arange(SK)[None, :]
    m = np.where((j >= QT) | (j <= i), 0.0, -1e30)
    r["s_mask"] = np.tile(m, (2, 4)).astype(NP_BF16)
    return r


def segment_arrays(g_norm, W_qkv, W_out, pm):
    swap = np.arange(P) ^ 1
    idx = []
    for hp in range(HP):
        for kind in range(2):
            base = kind * INNER + hp * P
            idx += [base + np.arange(P), base + swap]
    idx = np.concatenate(idx + [2 * INNER + np.arange(INNER)])
    wo = W_out.reshape(HP, P, DM).transpose(1, 0, 2).reshape(P, HP * DM)
    w = np.concatenate([W_qkv[:, idx], wo], 1)
    pmk = pm[0].reshape(HP, 2, PM, DH).transpose(1, 3, 0, 2).reshape(P, HP, PM)
    pmv = pm[1].transpose(1, 0, 2).reshape(PM, INNER)
    return w, g_norm[:, None], np.ascontiguousarray(pmk), np.ascontiguousarray(pmv)


def build_program(nc, d, out):
    with ExitStack() as ctx:
        X = ctx.enter_context(nc.sbuf_tensor("x", [P, NT], F32))
        C = make_consts(nc, ctx, d)
        C.d = d
        C.v_zero = ctx.enter_context(nc.semaphore("v_zero"))
        C.f_tab_d, C.f_mask_d = d["f_tab"], d["f_mask"]
        C.parts_s = nc.dram_tensor("parts_scratch", [2, 3, P, T], BF16, kind="Internal").ap()
        C.max_s = nc.dram_tensor("max_scratch", [3, P, P], BF16, kind="Internal").ap()

        S = Signals(nc, "x_in", "load_")
        with nc.Block() as block:
            @block.sync
            def _(sp):
                sp.dma_start(X[:, :], d["x"][:, :]).then_inc(S["x_in"], 16)
                sp.wait_ge(S["x_in"], 16)
        S.clear()
        S.close()

        C.stage += 1
        small_head_attention(nc, C, X, "rope", d["a0_w"], d["h_tab0"], d["a0_cols"], d["a0_brow"])
        C.stage += 1
        ffn_stack(nc, C, X, d["f_wa"], d["f_wb"], d["f_cc"])
        C.stage += 1
        small_head_attention(nc, C, X, "latent", d["b0_w"], d["h_tab1"], d["b0_cols"], d["b0_brow"])
        C.stage += 1
        ffn_stack(nc, C, X, d["f_wa"], d["f_wb"], d["f_cc"])
        C.stage += 1
        small_head_attention(nc, C, X, "plain", d["a1_w"], d["h_tab0"], d["a1_cols"], d["a1_brow"])
        C.stage += 1
        experts(nc, C, X, d["e_wg"], d["e_w1"], d["e_b1"], d["e_w2"], d["e_b2"])
        C.stage += 1
        segment_attention(nc, C, X, d["s_w"], d["s_g"], d["s_pmk"], d["s_pmv"])
        C.stage += 1
        experts(nc, C, X, d["e_wg"], d["e_w1"], d["e_b1"], d["e_w2"], d["e_b2"])

        S = Signals(nc, "x_out", "store_")
        with nc.Block() as block:
            @block.sync
            def _(sp):
                sp.dma_start(out[:, :], X[:, :]).then_inc(S["x_out"], 16)
                sp.wait_ge(S["x_out"], 16)
        S.close()


def kernel(**inputs):
    import concourse.bacc as bacc
    from concourse.bass_utils import run_bass_kernel_spmd

    a = {k: np.asarray(v) for k, v in inputs.items()}

    def of(prefix, names):
        return [a[prefix + n] for n in names.split()]

    arrays = {"x": a["L0_attn_a_x"].reshape(NT, DM).T}
    arrays["a0_w"], arrays["a0_cols"], arrays["a0_brow"] = rope_arrays(*of("L0_attn_a_", "W_qkv W_out"))
    arrays["b0_w"], arrays["b0_cols"], arrays["b0_brow"] = latent_arrays(
        *of("L0_attn_b_", "Wd_q_w Wd_q_b Wu_q_w Wu_q_b Wq_r_w Wq_r_b Wk_r_w Wk_r_b Wd_kv_w Wd_kv_b "
                          "Wu_k_w Wu_k_b Wu_v_w Wu_v_b Wo_w Wo_b"))
    arrays["a1_w"], arrays["a1_cols"], arrays["a1_brow"] = plain_arrays(*of("L1_attn_a_", "WQ WK WV WO"))
    arrays["f_wa"], arrays["f_wb"], arrays["f_cc"] = ffn_arrays(
        *of("L0_ffn_", "Wqkv q_scale k_scale Wo ln_g ln_b W1 b1 W2 b2"))
    arrays["e_wg"], arrays["e_w1"], arrays["e_b1"], arrays["e_w2"], arrays["e_b2"] = expert_arrays(
        *of("L1_ffn_", "Wg W1 b1 W2 b2"))
    arrays["s_w"], arrays["s_g"], arrays["s_pmk"], arrays["s_pmv"] = segment_arrays(
        *of("L1_attn_b_", "g_norm W_qkv W_out pm"))
    arrays.update(const_arrays())
    arrays.update(head_const_arrays())
    arrays.update(expert_const_arrays())
    arrays.update(segment_const_arrays())

    nc = bacc.Bacc("TRN2", target_bir_lowering=False, num_devices=1)
    arrays = {f"in_{k}": np.ascontiguousarray(v) for k, v in arrays.items()}
    d = {k[3:]: nc.dram_tensor(k, v.shape, mybir.dt.from_np(v.dtype), kind="ExternalInput").ap() for k, v in arrays.items()}
    out = nc.dram_tensor("out", [P, NT], F32, kind="ExternalOutput").ap()
    build_program(nc, d, out)
    r = run_bass_kernel_spmd(nc, [arrays], core_ids=[0])
    return np.ascontiguousarray(r.results[0]["out"].T).reshape(BATCH, T, DM)
```
